# Optimizing a Trainium2 kernel written in Bass

```python
import numpy as np
import jax
import jax.numpy as jnp

def _softmax(x, axis=-1):
    return jax.nn.softmax(x, axis=axis)

def _gelu(x):
    return jax.nn.gelu(x, approximate=True)

def _silu(x):
    return jax.nn.silu(x)

def _sigmoid(x):
    return jax.nn.sigmoid(x)

def _layernorm(x, axis=-1, eps=1e-05):
    m = jnp.mean(x, axis=axis, keepdims=True)
    v = jnp.var(x, axis=axis, keepdims=True)
    return (x - m) / jnp.sqrt(v + eps)

def _scatter_add(tgt, idx, src, axis=0):
    return tgt.at[idx].add(src)

def _segment_sum(src, seg, n):
    return jax.ops.segment_sum(src, seg, n)
kernel_name = 'mk_hybrid_d1_jaxref_r4_7b71c8'

def setup_inputs(seed: int=0):
    np.random.seed(seed)
    _w = jnp.asarray

    def _L0_attn_a_setup():
        import jax, jax.numpy as jnp
        import numpy as np
        EMBED = 256
        HEADS = 16
        HEAD_DIM = EMBED // HEADS
        key = jax.random.key(seed)
        k1, k2, k3, k4, k5 = jax.random.split(key, 5)
        scale = 1.0 / np.sqrt(EMBED)
        return {'x': jax.random.normal(k1, (4, 512, EMBED), dtype=jnp.float32), 'qkv_w': jax.random.uniform(k2, (3 * EMBED, EMBED), minval=-scale, maxval=scale, dtype=jnp.float32), 'qkv_b': jax.random.uniform(k3, (3 * EMBED,), minval=-scale, maxval=scale, dtype=jnp.float32), 'out_w': jax.random.uniform(k4, (EMBED, EMBED), minval=-scale, maxval=scale, dtype=jnp.float32), 'out_b': jax.random.uniform(k5, (EMBED,), minval=-scale, maxval=scale, dtype=jnp.float32)}
    _L0_attn_a_in = _L0_attn_a_setup()

    def _L0_attn_b_setup():
        import jax, jax.numpy as jnp
        import numpy as np
        D_MODEL = 256
        NUM_HEADS = 16
        D_K = D_MODEL // NUM_HEADS
        MAX_SEQ_LEN = 1024
        THETA = 10000.0

        def _rope_tables(seq_len):
            pos = jnp.arange(seq_len, dtype=jnp.float32)
            pair = jnp.arange(D_K // 2, dtype=jnp.float32)
            rates = THETA ** (-(2.0 * pair) / D_K)
            angles = pos[:, None] * rates[None, :]
            return (jnp.cos(angles), jnp.sin(angles))

        def _apply_rope(x, cos, sin):
            x_even = x[..., 0::2]
            x_odd = x[..., 1::2]
            r_even = x_even * cos - x_odd * sin
            r_odd = x_even * sin + x_odd * cos
            out = jnp.stack([r_even, r_odd], axis=-1)
            return out.reshape(x.shape)
        key = jax.random.key(seed)
        ks = jax.random.split(key, 5)
        x = jax.random.normal(ks[0], (1, 1024, D_MODEL), dtype=jnp.float32)
        Wq = jax.random.truncated_normal(ks[1], -2.0, 2.0, (D_MODEL, D_MODEL), dtype=jnp.float32) * D_MODEL ** (-0.5)
        Wk = jax.random.truncated_normal(ks[2], -2.0, 2.0, (D_MODEL, D_MODEL), dtype=jnp.float32) * D_MODEL ** (-0.5)
        Wv = jax.random.truncated_normal(ks[3], -2.0, 2.0, (D_MODEL, D_MODEL), dtype=jnp.float32) * D_MODEL ** (-0.5)
        Wo = jax.random.truncated_normal(ks[4], -2.0, 2.0, (D_MODEL, D_MODEL), dtype=jnp.float32) * D_MODEL ** (-0.5)
        return {'x': x, 'Wq': Wq, 'Wk': Wk, 'Wv': Wv, 'Wo': Wo}
    _L0_attn_b_in = _L0_attn_b_setup()

    def _L0_ffn_setup():
        import jax, jax.numpy as jnp
        import numpy as np
        D_MODEL = 256
        DEPTH = 8
        M = 2 ** DEPTH
        N_INTERNAL = M - 1
        B, T = (8, 1024)

        def _leaf_probs(gate):
            BT = gate.shape[0]
            lp = jnp.ones((BT, M), dtype=gate.dtype)
            for level in range(DEPTH):
                n = 2 ** level
                half = M // (2 * n)
                g = gate[:, n - 1:2 * n - 1]
                f = jnp.stack([1.0 - g, g], axis=-1)
                f = jnp.broadcast_to(f[..., None], (BT, n, 2, half))
                lp = lp * f.reshape(BT, M)
            return lp
        key = jax.random.key(seed)
        ks = jax.random.split(key, 7)
        x = jax.random.normal(ks[0], (B, T, D_MODEL), dtype=jnp.float32)
        Wq = jax.random.normal(ks[1], (D_MODEL, D_MODEL), dtype=jnp.float32) * 0.02
        routers = jax.random.normal(ks[2], (N_INTERNAL, D_MODEL), dtype=jnp.float32) * 0.02
        leaf_keys = jax.random.normal(ks[3], (M, D_MODEL), dtype=jnp.float32) * 0.02
        leaf_values = jax.random.normal(ks[4], (M, D_MODEL), dtype=jnp.float32) * 0.02
        Wout_w = jax.random.normal(ks[5], (D_MODEL, D_MODEL), dtype=jnp.float32) * 0.02
        Wout_b = jax.random.normal(ks[6], (D_MODEL,), dtype=jnp.float32) * 0.02
        return {'x': x, 'Wq': Wq, 'routers': routers, 'leaf_keys': leaf_keys, 'leaf_values': leaf_values, 'Wout_w': Wout_w, 'Wout_b': Wout_b}
    _L0_ffn_in = _L0_ffn_setup()
    _d = {'L0_attn_a_x': _L0_attn_a_in['x'], 'L0_attn_a_qkv_w': _L0_attn_a_in['qkv_w'], 'L0_attn_a_qkv_b': _L0_attn_a_in['qkv_b'], 'L0_attn_a_out_w': _L0_attn_a_in['out_w'], 'L0_attn_a_out_b': _L0_attn_a_in['out_b'], 'L0_attn_b_Wq': _L0_attn_b_in['Wq'], 'L0_attn_b_Wk': _L0_attn_b_in['Wk'], 'L0_attn_b_Wv': _L0_attn_b_in['Wv'], 'L0_attn_b_Wo': _L0_attn_b_in['Wo'], 'L0_ffn_Wq': _L0_ffn_in['Wq'], 'L0_ffn_routers': _L0_ffn_in['routers'], 'L0_ffn_leaf_keys': _L0_ffn_in['leaf_keys'], 'L0_ffn_leaf_values': _L0_ffn_in['leaf_values'], 'L0_ffn_Wout_w': _L0_ffn_in['Wout_w'], 'L0_ffn_Wout_b': _L0_ffn_in['Wout_b']}
    _x0 = _d['L0_attn_a_x']
    _d['L0_attn_a_x'] = jax.random.normal(jax.random.fold_in(jax.random.key(seed), 1), (8, 512, 256), dtype=_x0.dtype)
    del _x0
    return _d

def reference(L0_attn_a_x, L0_attn_a_qkv_w, L0_attn_a_qkv_b, L0_attn_a_out_w, L0_attn_a_out_b, L0_attn_b_Wq, L0_attn_b_Wk, L0_attn_b_Wv, L0_attn_b_Wo, L0_ffn_Wq, L0_ffn_routers, L0_ffn_leaf_keys, L0_ffn_leaf_values, L0_ffn_Wout_w, L0_ffn_Wout_b):

    def _L0_attn_a_ref(x, qkv_w, qkv_b, out_w, out_b):
        import jax, jax.numpy as jnp
        import numpy as np
        EMBED = 256
        HEADS = 16
        HEAD_DIM = EMBED // HEADS
        b, n, _ = x.shape
        qkv = (jnp.einsum('bne,fe->bnf', x, qkv_w) + qkv_b).reshape(b, n, 3, HEADS, HEAD_DIM)
        q, k, v = (qkv[:, :, 0], qkv[:, :, 1], qkv[:, :, 2])
        scores = jnp.einsum('bnhd,bmhd->bhnm', q, k) / jnp.sqrt(jnp.float32(HEAD_DIM))
        attn = jax.nn.softmax(scores, axis=-1)
        out = jnp.einsum('bhnm,bmhd->bnhd', attn, v).reshape(b, n, EMBED)
        return jnp.einsum('bne,fe->bnf', out, out_w) + out_b

    def _L0_attn_b_ref(x, Wq, Wk, Wv, Wo):
        import jax, jax.numpy as jnp
        import numpy as np
        D_MODEL = 256
        NUM_HEADS = 16
        D_K = D_MODEL // NUM_HEADS
        MAX_SEQ_LEN = 1024
        THETA = 10000.0

        def _rope_tables(seq_len):
            pos = jnp.arange(seq_len, dtype=jnp.float32)
            pair = jnp.arange(D_K // 2, dtype=jnp.float32)
            rates = THETA ** (-(2.0 * pair) / D_K)
            angles = pos[:, None] * rates[None, :]
            return (jnp.cos(angles), jnp.sin(angles))

        def _apply_rope(x, cos, sin):
            x_even = x[..., 0::2]
            x_odd = x[..., 1::2]
            r_even = x_even * cos - x_odd * sin
            r_odd = x_even * sin + x_odd * cos
            out = jnp.stack([r_even, r_odd], axis=-1)
            return out.reshape(x.shape)
        b, s, _ = x.shape

        def split_heads(t):
            return t.reshape(b, s, NUM_HEADS, D_K).transpose(0, 2, 1, 3)
        q = split_heads(x @ Wq.T)
        k = split_heads(x @ Wk.T)
        v = split_heads(x @ Wv.T)
        cos, sin = _rope_tables(s)
        q = _apply_rope(q, cos, sin)
        k = _apply_rope(k, cos, sin)
        scores = jnp.einsum('bhqd,bhkd->bhqk', q, k) / jnp.sqrt(jnp.float32(D_K))
        causal = jnp.tril(jnp.ones((s, s), dtype=bool))
        scores = jnp.where(causal, scores, jnp.float32(-1000000000.0))
        probs = jax.nn.softmax(scores, axis=-1)
        attn = jnp.einsum('bhqk,bhkd->bhqd', probs, v)
        attn = attn.transpose(0, 2, 1, 3).reshape(b, s, D_MODEL)
        return attn @ Wo.T

    def _L0_ffn_ref(x, Wq, routers, leaf_keys, leaf_values, Wout_w, Wout_b):
        import jax, jax.numpy as jnp
        import numpy as np
        D_MODEL = 256
        DEPTH = 8
        M = 2 ** DEPTH
        N_INTERNAL = M - 1
        B, T = (8, 1024)

        def _leaf_probs(gate):
            BT = gate.shape[0]
            lp = jnp.ones((BT, M), dtype=gate.dtype)
            for level in range(DEPTH):
                n = 2 ** level
                half = M // (2 * n)
                g = gate[:, n - 1:2 * n - 1]
                f = jnp.stack([1.0 - g, g], axis=-1)
                f = jnp.broadcast_to(f[..., None], (BT, n, 2, half))
                lp = lp * f.reshape(BT, M)
            return lp
        Bv, Tv, d = x.shape
        q = jnp.einsum('btd,ed->bte', x, Wq)
        q_flat = q.reshape(Bv * Tv, d)
        gate = jax.nn.sigmoid(q_flat @ routers.T)
        leaf_prob = _leaf_probs(gate)
        ret = (leaf_prob @ leaf_values).reshape(Bv, Tv, d)
        return jnp.einsum('btd,ed->bte', ret, Wout_w) + Wout_b
    x = L0_attn_a_x
    x = x + _L0_attn_a_ref(_layernorm(x, axis=-1), L0_attn_a_qkv_w, L0_attn_a_qkv_b, L0_attn_a_out_w, L0_attn_a_out_b)
    x = x + _L0_ffn_ref(_layernorm(x, axis=-1), L0_ffn_Wq, L0_ffn_routers, L0_ffn_leaf_keys, L0_ffn_leaf_values, L0_ffn_Wout_w, L0_ffn_Wout_b)
    x = x + _L0_attn_b_ref(_layernorm(x, axis=-1), L0_attn_b_Wq, L0_attn_b_Wk, L0_attn_b_Wv, L0_attn_b_Wo)
    x = x + _L0_ffn_ref(_layernorm(x, axis=-1), L0_ffn_Wq, L0_ffn_routers, L0_ffn_leaf_keys, L0_ffn_leaf_values, L0_ffn_Wout_w, L0_ffn_Wout_b)
    return x

_drawn_inputs = setup_inputs


def setup_inputs(seed=0):
    import zlib

    import numpy as np

    out = dict(_drawn_inputs(seed))
    spreads = {}
    factors = {'L0_ffn_Wq': 8.0, 'L0_ffn_routers': 8.0, 'L0_ffn_leaf_values': 8.0, 'L0_ffn_Wout_w': 8.0}
    for name, (base, spread) in spreads.items():
        noise = np.random.default_rng([zlib.crc32(name.encode()), seed]).standard_normal(out[name].shape)
        drawn = base * np.exp(spread * noise) if base else spread * noise
        out[name] = jnp.asarray(drawn.astype(out[name].dtype))
    for name, factor in factors.items():
        out[name] = (out[name] * factor).astype(out[name].dtype)
    return out
```

```python
from contextlib import ExitStack

import numpy as np

import concourse.bass as bass
from concourse import mybir

F32 = mybir.dt.float32
BF16 = mybir.dt.bfloat16
ALU = mybir.AluOpType
ACT = mybir.ActivationFunctionType
AX_X = mybir.AxisListType.X

P = 128
BATCH, T, D = 8, 512, 256
HEADS = 16
DH = D // HEADS
PAIRS = DH // 2
TILES = T // P
KC = D // P
LEVELS = 8
LEAVES = 2 ** LEVELS
NODES = LEAVES - 1
EPS = 1e-5
THETA = 10000.0
SCALE = float(DH) ** -0.5
MASKED = -1e30
DMA = 16

GROUP = 4
GROUPS = HEADS // GROUP
COLS = 32
VALUE = DH + 1

QUERY_PARTS = (0, 0, 0, 1, 1, 2)
KEY_PARTS = (0, 1, 2, 0, 1, 0)
SPLIT_ROWS = len(QUERY_PARTS) * DH
SHIFT_ROW = SPLIT_ROWS
STACK_ROWS = SPLIT_ROWS + 1
STACK_DMAS = 2 * 2 * len(QUERY_PARTS)

STEPS = GROUPS * TILES
SLOTS = STEPS * GROUP
LEAD = 24
SHIFT_LAG = 4
RING = 4
SCORE_BANKS = 3

PHASES = 2 * BATCH
LOOP_FIRST, LOOP_PHASES = 2, 2
TURNS = (PHASES - 2 - LOOP_FIRST) // LOOP_PHASES

FINISH = (
    (2, "residual", 0), (5, "turn_attended", 0), (6, "turn_attended", 1), (8, "project_out", 0),
    (10, "project_out", 1), (27, "moments", 0), (29, "normalize", 0), (31, "turn_normed", 0),
    (33, "turn_normed", 1), (35, "gates", 0), (37, "gates", 1), (38, "leaves", 0), (39, "leaves", 1),
    (41, "leaves", 2), (43, "leaves", 3), (46, "turn_leaves", 0), (48, "turn_leaves", 1), (50, "mix", 0),
    (53, "mix", 1),
)
PREPARE = (
    (1, "moments", 0), (3, "normalize", 0), (12, "turn_normed", 0), (13, "turn_normed", 1),
    (15, "heads_k", 0), (16, "heads_k", 1), (17, "rotate_k", 0), (17, "parts_k", 0), (18, "values", 0),
    (19, "values", 1), (21, "heads_q", 0), (23, "heads_q", 1), (24, "rotate_q", 0), (24, "parts_q", 0),
)
FINISH_FIRST = (
    (2, "residual", 0), (5, "turn_attended", 0), (6, "turn_attended", 1), (7, "project_out", 0),
    (8, "project_out", 1), (9, "moments", 0), (10, "normalize", 0), (11, "turn_normed", 0),
    (12, "turn_normed", 1), (13, "gates", 0), (14, "gates", 1), (15, "leaves", 0), (15, "leaves", 1),
    (16, "leaves", 2), (17, "leaves", 3), (18, "turn_leaves", 0), (19, "turn_leaves", 1), (20, "mix", 0),
    (21, "mix", 1),
)
PREPARE_LAST = (
    (22, "moments", 0), (23, "normalize", 0), (24, "turn_normed", 0), (25, "turn_normed", 1),
    (26, "heads_k", 0), (27, "heads_k", 1), (28, "rotate_k", 0), (28, "parts_k", 0), (29, "values", 0),
    (30, "values", 1), (31, "heads_q", 0), (32, "heads_q", 1), (33, "rotate_q", 0), (33, "parts_q", 0),
)
LEAF_LEVELS = ((0, 1, 2, 3), (4, 5), (6,), (7,))

PER_TURN = dict(
    scores_full=2 * 64, max_done=2 * 64, shift_full=2 * 4, shift_row=2 * 4, shift_sent0=2 * 2, shift_sent1=2 * 2,
    keyed_full=2 * 64, exp_done=2 * 64, causal_done=16, mixed_done=2 * 16, out_ready=2 * 4,
    out_turned=2 * 4, inverse_done=2 * 4, attended=2 * 4,
    moments_done=2 * 2, spread_done=2 * 2, variance=2 * 2, rstd=2 * 2, normed=2 * 2, turned_full=2 * 8,
    turned=2 * 8, added_full=2 * 4, x_ready=2 * 4, biased=2 + 1, gates_full=2 * 2, gates=2 * 2, level_done=2 * 8,
    heads_full=2 * 4, raw_ready=4, product_done=2, rotated=4, high=2 * 4, rest=2 * 4, middle=2 * 2, low=2 * 2,
    values_full=2 * 2, values_ready=2 * 2,
    stacked0=STACK_DMAS, stacked1=STACK_DMAS, x_loaded=1, x_again=1, kept=1, stored=1,
)


def causal(n):
    return n == PHASES - 1 or (n > 0 and n % 2 == 0)


def element(n):
    return BATCH - 1 if n == PHASES - 1 else n // 2 - 1 if causal(n) else (n + 1) // 2


def schedule(n):
    apart = n > 0 and n + 1 < PHASES and element(n - 1) == element(n + 1)
    due = {}
    if n > 0:
        for slot, step, i in FINISH_FIRST if apart else FINISH:
            due.setdefault(slot, []).append((step, i, n - 1))
    if n + 1 < PHASES:
        for slot, step, i in PREPARE_LAST if apart else PREPARE:
            due.setdefault(slot, []).append((step, i, n + 1))
    return due


def score_unit(n, slot):
    n, unit = n + (slot + LEAD) // SLOTS, (slot + LEAD) % SLOTS
    return n, unit, unit // 16, unit % 16 // TILES, unit % TILES


def shift_due(n, unit):
    return unit % 16 == SHIFT_LAG and 16 < n * SLOTS + unit < PHASES * SLOTS + 16


class Count:

    def __init__(self):
        self.n = dict.fromkeys(PER_TURN, 0)
        self.turn = None

    def add(self, event, times=1):
        self.n[event] += times

    def some(self, event, back=0):
        return self.turn is not None or self.n[event] > back

    def of(self, event, back=0):
        n = self.n[event] - back
        return n if self.turn is None else self.turn * PER_TURN[event] + n

    def next(self, event):
        self.add(event)
        return self.of(event)

    def enter(self, turn):
        self.turn, self.start = turn, dict(self.n)

    def leave(self):
        self.turn = None
        for event, n in self.n.items():
            grown = n - self.start[event]
            assert grown in (0, PER_TURN[event]), (event, grown, PER_TURN[event])
            self.n[event] += grown * (TURNS - 1)


def build(nc, x, w, out):
    with ExitStack() as ctx:
        def sb(name, shape, dt=F32):
            return ctx.enter_context(nc.sbuf_tensor(name, shape, dt))

        def bank(name, shape):
            return ctx.enter_context(nc.psum_tensor(name, shape, F32))

        def sem(name):
            return ctx.enter_context(nc.semaphore(name))

        weights = {k: sb(k, [P, KC, D]) for k in ("a_q", "a_k", "a_v", "a_o", "b_q", "b_k", "b_v", "b_o")}
        gate_w = sb("gate_w", [P, KC, D])
        leaf_w = sb("leaf_w", [P, KC, D])
        head_bias = {k: sb(k, [P, 2]) for k in ("a_q_bias", "a_k_bias")}
        wide_bias = {k: sb(k, [P, D]) for k in ("a_v_bias", "a_o_bias", "ffn_bias")}
        cosine = sb("cosine", [P, T])
        sine = sb("sine", [P, T])
        ident = sb("ident", [P, P])
        ident_b = sb("ident_b", [P, P], BF16)
        mask_b = sb("mask_b", [P, P], BF16)
        minus_half = sb("minus_half", [P, TILES])

        x_in = sb("x_in", [P, TILES, D])
        x_again = sb("x_again", [P, TILES, D])
        x_plain = sb("x_plain", [P, TILES, D])
        x_kept = sb("x_kept", [P, TILES, D])
        x_causal = sb("x_causal", [P, TILES, D])

        q_stack = [sb(f"q_stack{s}", [P, HEADS, T], BF16) for s in range(2)]
        k_stack = [sb(f"k_stack{s}", [P, HEADS, T], BF16) for s in range(2)]
        v_flat = [sb(f"v_ones{s}", [P, TILES * HEADS * VALUE + COLS - VALUE]) for s in range(2)]

        def values_of(s):
            return v_flat[s][:, 0:TILES * HEADS * VALUE].rearrange("p (t h d) -> p t h d", t=TILES, h=HEADS)

        turned = sb("turned", [P, KC, T])
        attended = sb("attended", [P, TILES, D])
        parts = {k: [sb(f"{k}_part{i}", [P, 2, T], BF16) for i in range(3)] for k in "qk"}
        scratch = sb("scratch", [P, 5, 1024])
        probs = [sb(f"probs{i}", [P, GROUP, T]) for i in range(RING)]
        out_raw = [sb(f"out_raw{i}", [P, T]) for i in range(2)]
        neg_max = [sb(f"neg_max{i}", [P, TILES, GROUP], BF16) for i in range(2)]
        shift_rows = [sb(f"shift_rows{i}", [GROUP, T], BF16) for i in range(2)]
        inverse = sb("inverse", [P, TILES, GROUP])
        moments = sb("moments", [P, TILES, 6])
        spread = sb("spread", [P, TILES, 2])
        variance = sb("variance", [P, TILES])
        rstd = sb("rstd", [P, TILES])

        def tiles_of(i):
            return scratch[:, i, :].rearrange("p (t n) -> p t n", t=TILES)

        def halves_of(i):
            return scratch[:, i, :].rearrange("p (c n) -> p c n", c=2)

        def staged(i, n):
            return scratch[:, 1 + i // 2, 512 * (i % 2):512 * (i % 2) + KC * n].rearrange("p (k n) -> p k n", k=KC)

        normed, tanh_gates, leaf_probs = tiles_of(0), tiles_of(0), [tiles_of(1), tiles_of(2)]
        raw, by_cos, by_sin, rotated = (halves_of(i) for i in range(4))
        rest = halves_of(4)

        ps_max = [bank(f"ps_max{i}", [P, T]) for i in range(SCORE_BANKS)]
        ps_key = [bank(f"ps_key{i}", [P, T]) for i in range(2)]
        ps_out = bank("ps_out", [P, T])
        ps_turn = bank("ps_turn", [P, T])
        ps_work = bank("ps_work", [P, T])
        work_tiles = ps_work[:, :].rearrange("p (t n) -> p t n", t=2)
        turn_heads = ps_turn[:, :].rearrange("p (q j c) -> p q j c", q=TILES, j=GROUP)
        turn_shift = ps_turn[0:GROUP, 0:T // 2].bitcast(BF16)

        on = {name: sem(name) for name in PER_TURN}
        first_loaded = sem("first_loaded")
        rest_loaded = sem("rest_loaded")
        zeroed = sem("zeroed")
        constants = sem("constants")
        ones_set = sem("ones_set")
        fold_full = sem("fold_full")
        folded = sem("folded")
        FIRST = ("a_k", "a_q", "a_v", "a_k_bias", "a_q_bias", "a_v_bias")
        REST = ("a_o", "b_q", "b_k", "b_v", "b_o", "a_o_bias", "ffn_bias", "cosine", "sine",
                "ffn_q", "routers", "leaf_values", "ffn_o")
        block = ctx.enter_context(nc.Block())

        def load_weight(eng, name, loaded):
            by_rows = lambda ap: ap.rearrange("(k p) n -> p k n", p=P)
            if name in weights:
                dst, src = weights[name][:, :, :], by_rows(w[name])
            elif name in head_bias:
                dst, src = head_bias[name][:, :], w[name]
            elif name in wide_bias:
                dst, src = wide_bias[name][:, :], w[name].partition_broadcast(P)
            elif name in ("cosine", "sine"):
                dst, src = (cosine if name == "cosine" else sine)[:, :], w[name]
            else:
                at = ("ffn_q", "routers", "leaf_values", "ffn_o").index(name)
                dst, src = staged(at, w[name].shape[1]), by_rows(w[name])
            eng.dma_start(dst, src).then_inc(loaded, DMA)

        def program(eng, count, core, steps, opening, closing):
            def phase(n):
                due = schedule(n)
                for slot in range(SLOTS):
                    core(n, slot)
                    for step, i, m in due.get(slot, ()):
                        if step in steps:
                            steps[step](m, i, n)

            for _, step, i in PREPARE:
                if step in steps:
                    steps[step](0, i, -1)
            opening()
            for n in range(LOOP_FIRST):
                phase(n)
            with eng.Fori(0, TURNS) as turn:
                count.enter(turn)
                for n in range(LOOP_FIRST, LOOP_FIRST + LOOP_PHASES):
                    phase(n)
            count.leave()
            for n in range(LOOP_FIRST + TURNS * LOOP_PHASES, PHASES):
                phase(n)
            closing()
            for _, step, i in FINISH:
                if step in steps:
                    steps[step](PHASES - 1, i, PHASES)

        def stream(m, n):
            if n < m:
                return x_plain if causal(m) else x_in
            return x_causal if causal(m) else x_plain

        @block.sync
        def _(sp):
            count = Count()

            def one(tensor, e):
                got = tensor[e] if count.turn is None else tensor[bass.ds(count.turn + e, 1)].squeeze(0)
                return got.rearrange("(t p) d -> p t d", p=P)

            def load_x(m):
                if count.some("normed"):
                    sp.wait_ge(on["normed"], count.of("normed"))
                    sp.nop(nofuse=True)
                sp.dma_start(x_in[:, :, :], one(x, element(m))).then_inc(on["x_loaded"], DMA)

            def load_again(m):
                if count.some("x_ready"):
                    sp.wait_ge(on["x_ready"], count.of("x_ready"))
                    sp.nop(nofuse=True)
                sp.dma_start(x_again[:, :, :], one(x, element(m))).then_inc(on["x_again"], DMA)

            def core(n, slot):
                if slot == 0:
                    if n > 0:
                        count.add("keyed_full", SLOTS)
                    if n + 1 < PHASES and not causal(n + 1):
                        load_x(n + 1)
                if slot == 40 and not causal(n):
                    load_again(n)

            def stack(m, which, part):
                dst = (q_stack if which == "q" else k_stack)[m % 2]
                held = on["stacked0"] if m % 2 == 0 else on["stacked1"]
                for c in range(2):
                    for r, holds in enumerate(QUERY_PARTS if which == "q" else KEY_PARTS):
                        if holds == part:
                            row = DH * r + PAIRS * c
                            sp.dma_start(dst[row:row + PAIRS, :, :], parts[which][part][:, c, :]).then_inc(held, DMA)

            def parts_step(which):
                def step(m, i, n):
                    if count.some("keyed_full"):
                        sp.wait_ge(on["keyed_full"], count.of("keyed_full"))
                        sp.nop(nofuse=True)
                    count.add("high", 2)
                    sp.wait_ge(on["high"], count.of("high"))
                    sp.nop(nofuse=True)
                    stack(m, which, 0)
                    sp.wait_ge(on["middle"], count.next("middle"))
                    sp.nop(nofuse=True)
                    stack(m, which, 1)
                    sp.wait_ge(on["low"], count.next("low"))
                    sp.nop(nofuse=True)
                    stack(m, which, 2)
                return step

            def normalize(m, i, n):
                count.add("normed")

            def keep(m):
                sp.wait_ge(on["x_ready"], count.of("x_ready"))
                sp.nop(nofuse=True)
                sp.dma_start(x_kept[:, :, :], x_plain[:, :, :]).then_inc(on["kept"], DMA)

            def project_out(m, i, n):
                count.add("x_ready")
                if i == 1 and causal(m) and n < PHASES:
                    keep(m)

            def mix(m, i, n):
                count.add("x_ready")
                if i == 1 and m == 0:
                    keep(m)
                if i == 1 and causal(m):
                    sp.wait_ge(on["x_ready"], count.of("x_ready"))
                    sp.nop(nofuse=True)
                    sp.dma_start(one(out, element(m)), x_causal[:, :, :]).then_inc(on["stored"], DMA)
                    count.add("stored")

            def opening():
                pass

            sp.sem_inc(on["stored"], DMA)
            count.add("stored")
            load_x(0)
            for name in FIRST:
                load_weight(sp, name, first_loaded)
            program(sp, count, core, dict(parts_k=parts_step("k"), parts_q=parts_step("q"), normalize=normalize,
                                          project_out=project_out, mix=mix), opening, opening)
            sp.wait_ge(on["stored"], count.of("stored") * DMA)

        @block.gpsimd
        def _(pool):
            count = Count()
            for t in (ident, ident_b, mask_b):
                pool.memset(t[:, :], 0.0).then_inc(zeroed, 1)
            pool.memset(minus_half[:, :], -0.5).then_inc(zeroed, 1)
            for s in range(2):
                pool.memset(v_flat[s][:, TILES * HEADS * VALUE:], 0.0).then_inc(zeroed, 1)
                pool.memset(values_of(s)[:, :, :, DH:VALUE], 1.0).then_inc(constants, 1)
            pool.wait_ge(zeroed, 6)
            for t in (ident, ident_b):
                pool.affine_select(out=t[:, :], in_=t[:, :], compare_op=ALU.not_equal, fill=1.0, base=0,
                                   pattern=[[-1, P]], channel_multiplier=1).then_inc(constants, 1)
            pool.affine_select(out=mask_b[:, :], in_=mask_b[:, :], compare_op=ALU.is_ge, fill=MASKED, base=0,
                               pattern=[[-1, P]], channel_multiplier=1).then_inc(constants, 1)

            def send_shift(n, slot):
                n, unit, g, _, _ = score_unit(n, slot)
                if not shift_due(n, unit):
                    return
                n, g = (n, g - 1) if g else (n - 1, GROUPS - 1)
                pool.wait_ge(on["shift_row"], count.next("shift_row"))
                pool.nop(nofuse=True)
                sent = on["shift_sent0"] if g % 2 == 0 else on["shift_sent1"]
                pool.dma_start(q_stack[n % 2][SHIFT_ROW:STACK_ROWS, GROUP * g:GROUP * (g + 1), :],
                               shift_rows[g % 2][:, :]).then_inc(sent, DMA)

            def core(n, slot):
                send_shift(n, slot)
                step, r = slot // 4, slot % 4
                if r == 3:
                    count.add("exp_done", GROUP)
                    if causal(n):
                        kb = step % TILES
                        tile = probs[step % RING][:, :, P * kb:P * kb + P]
                        pool.wait_ge(on["exp_done"], count.of("exp_done"))
                        pool.nop(nofuse=True)
                        pool.affine_select(out=tile, in_=tile, compare_op=ALU.is_ge, fill=0.0, base=0,
                                           pattern=[[0, GROUP], [1, P]], channel_multiplier=-1)\
                            .then_inc(on["causal_done"], 1)

            def add_bias(dst, bias):
                row = wide_bias[bias][:, :].unsqueeze(1).broadcast_to([P, TILES, D])
                pool.tensor_tensor(dst[:, :, :], dst[:, :, :], row, ALU.add).then_inc(on["biased"], 1)

            def residual(m, i, n):
                if not causal(m):
                    pool.wait_ge(on["x_again"], count.next("x_again") * DMA)
                    pool.nop(nofuse=True)
                    add_bias(x_again, "a_o_bias")

            def moments_step(m, i, n):
                pool.wait_ge(on["variance"], count.next("variance"))
                pool.nop(nofuse=True)
                pool.tensor_tensor(rstd[:, :], variance[:, :], minus_half[:, :], ALU.pow).then_inc(on["rstd"], 1)

            def normalize(m, i, n):
                count.add("normed")
                if n >= m:
                    pool.wait_ge(on["normed"], count.of("normed"))
                    pool.nop(nofuse=True)
                    add_bias(stream(m, n), "ffn_bias")

            def low_part(which):
                def step(m, i, n):
                    pool.wait_ge(on["middle"], count.next("middle"))
                    pool.nop(nofuse=True)
                    pool.tensor_tensor(parts[which][2][:, :, :], rest, parts[which][1][:, :, :], ALU.subtract)\
                        .then_inc(on["low"], 1)
                return step

            def opening():
                pool.wait_ge(rest_loaded, DMA * len(REST))
                for slot in range(-LEAD, 0):
                    send_shift(0, slot)

            def closing():
                pass

            program(pool, count, core, dict(residual=residual, moments=moments_step, normalize=normalize,
                                            parts_k=low_part("k"), parts_q=low_part("q")), opening, closing)

        @block.scalar
        def _(act):
            count = Count()
            for name in REST:
                load_weight(act, name, rest_loaded)
            act.wait_ge(first_loaded, DMA * len(FIRST))

            def core(n, slot):
                step, j = slot // GROUP, slot % GROUP
                kb = step % TILES
                q0 = P * kb if causal(n) else 0
                if j == 0:
                    if count.some("mixed_done", RING - 1):
                        act.wait_ge(on["mixed_done"], count.of("mixed_done", RING - 1))
                    count.add("mixed_done")
                act.wait_ge(on["keyed_full"], count.next("keyed_full"))
                act.activation(probs[step % RING][:, j, q0:T], ps_key[slot % 2][:, 0:T - q0], ACT.Exp,
                               scale=SCALE).then_inc(on["exp_done"], 1)
                if j == 3 and kb == 0 and (n > 0 or step > 0):
                    copy_out(step // TILES - 1)

            def copy_out(g):
                act.wait_ge(on["mixed_done"], count.of("mixed_done", 1))
                act.activation(out_raw[g % 2][:, :], ps_out[:, :], ACT.Copy).then_inc(on["out_ready"], 1)

            def opening():
                pass

            def closing():
                count.add("mixed_done")
                copy_out(GROUPS - 1)

            def turn(m, i, n):
                act.wait_ge(on["turned_full"], count.next("turned_full"))
                act.activation(turned[:, i, :], ps_work[:, :], ACT.Copy).then_inc(on["turned"], 1)

            def gates(m, i, n):
                act.wait_ge(on["gates_full"], count.next("gates_full"))
                act.activation(tanh_gates[:, 2 * i:2 * i + 2, 0:NODES], work_tiles[:, :, 0:NODES], ACT.Tanh,
                               scale=0.5).then_inc(on["gates"], 1)

            def heads(which):
                def step(m, i, n):
                    act.wait_ge(on["heads_full"], count.next("heads_full"))
                    if causal(m):
                        act.activation(raw[:, i, :], ps_work[:, :], ACT.Copy).then_inc(on["raw_ready"], 1)
                    else:
                        act.activation(parts[which][0][:, i, :], ps_work[:, :], ACT.Identity,
                                       bias=head_bias[f"a_{which}_bias"][:, i:i + 1]).then_inc(on["high"], 1)
                return step

            def rotate(which):
                def step(m, i, n):
                    if causal(m):
                        for c in range(2):
                            act.wait_ge(on["rotated"], count.next("rotated"))
                            act.activation(parts[which][0][:, c, :], rotated[:, c, :], ACT.Copy)\
                               .then_inc(on["high"], 1)
                return step

            def middle_part(which):
                def step(m, i, n):
                    count.add("rest", 2)
                    act.wait_ge(on["rest"], count.of("rest"))
                    act.activation(parts[which][1][:, :, :], rest, ACT.Copy).then_inc(on["middle"], 1)
                return step

            program(act, count, core, dict(turn_attended=turn, turn_normed=turn, turn_leaves=turn, gates=gates,
                                           heads_k=heads("k"), heads_q=heads("q"), rotate_k=rotate("k"),
                                           rotate_q=rotate("q"), parts_k=middle_part("k"),
                                           parts_q=middle_part("q")), opening, closing)

        @block.vector
        def _(dve):
            count = Count()
            for s in range(2):
                dve.memset(k_stack[s][SHIFT_ROW:STACK_ROWS, :, :], 1.0).then_inc(ones_set, 1)
            dve.wait_ge(first_loaded, DMA * len(FIRST))

            def largest(n, slot):
                n, unit, g, j, qt = score_unit(n, slot)
                if n < PHASES:
                    keys = P * (qt + 1) if causal(n) else T
                    dve.wait_ge(on["scores_full"], count.next("scores_full"))
                    dve.tensor_reduce(out=neg_max[g % 2][:, qt, j:j + 1], in_=ps_max[unit % SCORE_BANKS][:, 0:keys],
                                      axis=AX_X, op=ALU.max, negate=True).then_inc(on["max_done"], 1)
                if shift_due(n, unit):
                    h = (g + 1) % 2
                    sent = on["shift_sent0"] if h == 0 else on["shift_sent1"]
                    dve.wait_ge(on["shift_full"], count.next("shift_full"))
                    if count.some(f"shift_sent{h}"):
                        dve.wait_ge(sent, count.of(f"shift_sent{h}") * DMA)
                    count.add(f"shift_sent{h}")
                    dve.tensor_copy(shift_rows[h][:, :], turn_shift).then_inc(on["shift_row"], 1)

            def divide(g):
                dve.wait_ge(on["out_turned"], count.next("out_turned"))
                dve.reciprocal(inverse[:, :, :], turn_heads[:, :, :, DH]).then_inc(on["inverse_done"], 1)
                dve.wait_ge(on["inverse_done"], count.next("inverse_done"))
                dst = attended[:, :, GROUP * DH * g:GROUP * DH * (g + 1)].rearrange("p q (j d) -> p q j d", j=GROUP)
                dve.tensor_tensor(dst, turn_heads[:, :, :, 0:DH],
                                  inverse[:, :, :].unsqueeze(3).broadcast_to([P, TILES, GROUP, DH]), ALU.mult)\
                   .then_inc(on["attended"], 1)

            def core(n, slot):
                largest(n, slot)
                step = slot // GROUP
                if slot % GROUP == 0 and step % TILES == 1 and (n > 0 or step > 1):
                    divide((step // TILES - 1) % GROUPS)

            def opening():
                dve.wait_ge(rest_loaded, DMA * len(REST))
                dve.wait_ge(fold_full, 1)
                for c in range(KC):
                    dve.tensor_copy(gate_w[:, c, 0:NODES], ps_max[c][:, 0:NODES]).then_inc(folded, 1)
                    dve.tensor_scalar(leaf_w[:, c, :], ps_key[c][:, 0:D], 2.0 ** -LEVELS, None, ALU.mult)\
                       .then_inc(folded, 1)
                for slot in range(-LEAD, 0):
                    largest(0, slot)

            def closing():
                divide(GROUPS - 1)

            def add(m, i, n, src):
                two = slice(2 * i, 2 * i + 2)
                dst = x_causal if causal(m) else x_plain
                dve.wait_ge(on["added_full"], count.next("added_full"))
                dve.tensor_tensor(dst[:, two, :], work_tiles, src[:, two, :], ALU.add).then_inc(on["x_ready"], 1)
                count.add("x_ready")

            def residual(m, i, n):
                if causal(m):
                    dve.wait_ge(on["kept"], count.next("kept") * DMA)
                    dve.wait_ge(on["stored"], count.next("stored") * DMA)
                else:
                    dve.wait_ge(on["biased"], count.next("biased"))
                    if count.some("kept"):
                        dve.wait_ge(on["kept"], count.of("kept") * DMA)

            def project_out(m, i, n):
                if i == 0:
                    residual(m, i, n)
                add(m, i, n, x_kept if causal(m) else x_again)

            def mix(m, i, n):
                if i == 0:
                    dve.wait_ge(on["biased"], count.next("biased"))
                add(m, i, n, stream(m, n))

            def moments_step(m, i, n):
                src = stream(m, n)
                if src is x_in:
                    dve.wait_ge(on["x_loaded"], count.next("x_loaded") * DMA)
                else:
                    dve.wait_ge(on["x_ready"], count.of("x_ready"))
                for t in range(TILES):
                    last = dve.bn_stats(moments[:, t, :], src[:, t, :])
                last.then_inc(on["moments_done"], 1)
                dve.wait_ge(on["moments_done"], count.next("moments_done"))
                dve.nop(nofuse=True)
                for t in range(TILES):
                    last = dve.bn_aggr(spread[:, t, :], moments[:, t, :])
                last.then_inc(on["spread_done"], 1)
                dve.wait_ge(on["spread_done"], count.next("spread_done"))
                dve.tensor_scalar(variance[:, :], spread[:, :, 1], EPS, None, ALU.add).then_inc(on["variance"], 1)

            def normalize(m, i, n):
                src = stream(m, n)
                dve.wait_ge(on["rstd"], count.next("rstd"))
                for t in range(TILES):
                    last = dve.tensor_scalar(normed[:, t, :], src[:, t, :], spread[:, t, 0:1], rstd[:, t:t + 1],
                                             ALU.subtract, ALU.mult)
                last.then_inc(on["normed"], 1)

            def leaves(m, i, n):
                if i == 0:
                    count.add("gates", 2)
                    dve.wait_ge(on["gates"], count.of("gates"))
                for level in LEAF_LEVELS[i]:
                    nodes = 2 ** level
                    gate = tanh_gates[:, :, nodes - 1:2 * nodes - 1]
                    above = leaf_probs[(level + 1) % 2][:, :, 0:nodes]
                    below = leaf_probs[level % 2][:, :, 0:2 * nodes].rearrange("p t (n s) -> p t n s", s=2)
                    if level == 0:
                        dve.tensor_scalar(below[:, :, :, 0], gate, -1.0, 1.0, ALU.mult, ALU.add)
                        last = dve.tensor_scalar(below[:, :, :, 1], gate, 1.0, None, ALU.add)
                    else:
                        dve.wait_ge(on["level_done"], count.of("level_done"))
                        dve.scalar_tensor_tensor(out=below[:, :, :, 0], in0=gate, scalar=1.0, in1=above,
                                                 op0=ALU.subtract, op1=ALU.mult, reverse0=True)
                        last = dve.scalar_tensor_tensor(out=below[:, :, :, 1], in0=gate, scalar=1.0, in1=above,
                                                        op0=ALU.add, op1=ALU.mult)
                    last.then_inc(on["level_done"], 1)
                    count.add("level_done")

            def rest_free(c):
                if c == 0 and count.some("low"):
                    dve.wait_ge(on["low"], count.of("low"))

            def heads(which):
                def step(m, i, n):
                    if causal(m):
                        return
                    dve.wait_ge(on["high"], count.next("high"))
                    rest_free(i)
                    dve.scalar_tensor_tensor(out=rest[:, i, :], in0=ps_work[:, :],
                                             scalar=head_bias[f"a_{which}_bias"][:, i:i + 1],
                                             in1=parts[which][0][:, i, :], op0=ALU.add, op1=ALU.subtract)\
                       .then_inc(on["rest"], 1)
                return step

            def rotate(which):
                def step(m, i, n):
                    if not causal(m):
                        return
                    count.add("raw_ready", 2)
                    dve.wait_ge(on["raw_ready"], count.of("raw_ready"))
                    dve.tensor_tensor(by_cos, raw, cosine[:, :].unsqueeze(1).broadcast_to([P, 2, T]), ALU.mult)
                    dve.tensor_tensor(by_sin, raw, sine[:, :].unsqueeze(1).broadcast_to([P, 2, T]), ALU.mult)\
                       .then_inc(on["product_done"], 1)
                    dve.wait_ge(on["product_done"], count.next("product_done"))
                    dve.tensor_tensor(rotated[:, 0, :], by_cos[:, 0, :], by_sin[:, 1, :], ALU.subtract)\
                       .then_inc(on["rotated"], 1)
                    dve.tensor_tensor(rotated[:, 1, :], by_sin[:, 0, :], by_cos[:, 1, :], ALU.add)\
                       .then_inc(on["rotated"], 1)
                    for c in range(2):
                        dve.wait_ge(on["high"], count.next("high"))
                        rest_free(c)
                        dve.tensor_tensor(rest[:, c, :], rotated[:, c, :], parts[which][0][:, c, :], ALU.subtract)\
                           .then_inc(on["rest"], 1)
                return step

            def parts_step(m, i, n):
                count.add("low")

            def values(m, i, n):
                dst = values_of(m % 2)[:, 2 * i:2 * i + 2, :, 0:DH]
                src = work_tiles.rearrange("p t (h d) -> p t h d", h=HEADS)
                dve.wait_ge(on["values_full"], count.next("values_full"))
                if causal(m):
                    dve.tensor_copy(dst, src).then_inc(on["values_ready"], 1)
                else:
                    bias = wide_bias["a_v_bias"][:, :].rearrange("p (h d) -> p h d", h=HEADS).unsqueeze(1)
                    dve.tensor_tensor(dst, src, bias.broadcast_to([P, 2, HEADS, DH]), ALU.add)\
                       .then_inc(on["values_ready"], 1)

            program(dve, count, core, dict(project_out=project_out, mix=mix, moments=moments_step,
                                           normalize=normalize, leaves=leaves, heads_k=heads("k"),
                                           heads_q=heads("q"), rotate_k=rotate("k"), rotate_q=rotate("q"),
                                           parts_k=parts_step, parts_q=parts_step, values=values),
                    opening, closing)

        @block.tensor
        def _(pe):
            count = Count()
            turn_read, work_read = [], []

            def take_turn(event):
                for read in turn_read:
                    pe.wait_ge(on[read], count.of(read))
                turn_read[:] = [event]
                count.add(event)

            def take_work(event):
                for read in work_read:
                    pe.wait_ge(on[read], count.of(read))
                work_read[:] = [event]
                count.add(event)

            pe.wait_ge(constants, 5)
            pe.wait_ge(ones_set, 2)
            pe.wait_ge(first_loaded, DMA * len(FIRST))

            def scores(n, unit, g, j, qt):
                if unit == 0:
                    held = on["stacked0"] if n % 2 == 0 else on["stacked1"]
                    count.add(f"stacked{n % 2}", STACK_DMAS)
                    pe.wait_ge(held, count.of(f"stacked{n % 2}") * DMA)
                h = GROUP * g + j
                keys = P * (qt + 1) if causal(n) else T
                back = 0 if unit == 0 else SCORE_BANKS if unit < SCORE_BANKS else SCORE_BANKS - 1
                if count.some("max_done", back):
                    pe.wait_ge(on["max_done"], count.of("max_done", back))
                count.add("max_done")
                dst = ps_max[unit % SCORE_BANKS]
                last = pe.matmul(dst[:, 0:keys], q_stack[n % 2][0:SPLIT_ROWS, h, P * qt:P * qt + P],
                                 k_stack[n % 2][0:SPLIT_ROWS, h, 0:keys], start=True, stop=not causal(n))
                if causal(n):
                    last = pe.matmul(dst[:, keys - P:keys], ident_b[:, :], mask_b[:, :], start=False, stop=True)
                last.then_inc(on["scores_full"], 1)

            def turn_max(g, begun):
                pe.wait_ge(on["max_done"], count.of("max_done", begun))
                take_turn("shift_row")
                for qt in range(TILES):
                    last = pe.transpose(turn_shift[:, P * qt:P * qt + P], neg_max[g % 2][:, qt, :], ident_b[:, :])
                last.then_inc(on["shift_full"], 1)

            def ahead(n, slot):
                n, unit, g, j, qt = score_unit(n, slot)
                if n < PHASES:
                    scores(n, unit, g, j, qt)
                if shift_due(n, unit):
                    turn_max((g - 1) % GROUPS, SHIFT_LAG + 1 if n < PHASES else 0)

            def by_key(n, slot):
                step, j = slot // GROUP, slot % GROUP
                g, kb = step // TILES, step % TILES
                q0 = P * kb if causal(n) else 0
                if kb == 0 and j == 0:
                    sent = on["shift_sent0"] if g % 2 == 0 else on["shift_sent1"]
                    pe.wait_ge(sent, count.next(f"shift_sent{g % 2}") * DMA)
                if count.some("exp_done", 1):
                    pe.wait_ge(on["exp_done"], count.of("exp_done", 1))
                count.add("exp_done")
                h = GROUP * g + j
                pe.matmul(ps_key[slot % 2][:, 0:T - q0], k_stack[n % 2][0:STACK_ROWS, h, P * kb:P * kb + P],
                          q_stack[n % 2][0:STACK_ROWS, h, q0:T], start=True, stop=True).then_inc(on["keyed_full"], 1)

            def mixed(n, step, begun):
                g, kb = step // TILES, step % TILES
                q0 = P * kb if causal(n) else 0
                if causal(n):
                    pe.wait_ge(on["causal_done"], count.next("causal_done"))
                else:
                    pe.wait_ge(on["exp_done"], count.of("exp_done", begun))
                if step == 0:
                    pe.wait_ge(on["values_ready"], count.of("values_ready"))
                if kb == 0:
                    if count.some("out_ready"):
                        pe.wait_ge(on["out_ready"], count.of("out_ready"))
                    count.add("out_ready")
                for j in range(GROUP):
                    at = VALUE * (HEADS * kb + GROUP * g + j)
                    last = pe.matmul(ps_out[COLS * j:COLS * j + COLS, q0:T], v_flat[n % 2][:, at:at + COLS],
                                     probs[step % RING][:, j, q0:T], start=(kb == 0), stop=(kb == TILES - 1),
                                     tile_position=(0, COLS * j))
                last.then_inc(on["mixed_done"], 1)

            def turn_out(g):
                pe.wait_ge(on["out_ready"], count.of("out_ready"))
                take_turn("attended")
                for qt in range(TILES):
                    last = pe.transpose(ps_turn[:, P * qt:P * qt + P], out_raw[g % 2][:, P * qt:P * qt + P], ident[:, :])
                last.then_inc(on["out_turned"], 1)

            def core(n, slot):
                step, r = slot // GROUP, slot % GROUP
                if n == LOOP_FIRST and slot == 0:
                    work_read[:] = ["raw_ready", "x_ready"]
                ahead(n, slot)
                if r == 0 and step % TILES == 1 and (n > 0 or step > 1):
                    turn_out((step // TILES - 1) % GROUPS)
                by_key(n, slot)
                if r == 2 and step > 0:
                    mixed(n, step - 1, 3)
                elif r == 2 and n > 0:
                    mixed(n - 1, STEPS - 1, 3)

            def opening():
                pe.wait_ge(rest_loaded, DMA * len(REST))
                for c in range(KC):
                    for k in range(KC):
                        pe.matmul(ps_max[c][:, 0:NODES], staged(0, D)[:, k, P * c:P * c + P],
                                  staged(1, NODES)[:, k, :], start=(k == 0), stop=(k == KC - 1))
                for c in range(KC):
                    for k in range(KC):
                        last = pe.matmul(ps_key[c][:, 0:D], staged(2, D)[:, k, P * c:P * c + P],
                                         staged(3, D)[:, k, :], start=(k == 0), stop=(k == KC - 1))
                last.then_inc(fold_full, 1)
                pe.wait_ge(folded, 4)
                for slot in range(-LEAD, 0):
                    ahead(0, slot)

            def closing():
                mixed(PHASES - 1, STEPS - 1, 0)
                turn_out(GROUPS - 1)

            def turn_tiles(src, i):
                take_work("turned")
                for t in range(TILES):
                    last = pe.transpose(ps_work[:, P * t:P * t + P], src[:, t, P * i:P * i + P], ident[:, :])
                last.then_inc(on["turned_full"], 1)

            def turn_attended(m, i, n):
                pe.wait_ge(on["attended"], count.of("attended"))
                turn_tiles(attended, i)

            def turn_normed(m, i, n):
                if i == 0:
                    pe.wait_ge(on["normed"], count.next("normed"))
                turn_tiles(normed, i)

            def turn_leaves(m, i, n):
                if i == 0:
                    count.add("level_done", LEVELS)
                    pe.wait_ge(on["level_done"], count.of("level_done"))
                turn_tiles(leaf_probs[(LEVELS - 1) % 2], i)

            def rows(weight, i, width, read):
                pe.wait_ge(on["turned"], count.of("turned"))
                take_work(read)
                for t in range(2):
                    tile = slice(P * (2 * i + t), P * (2 * i + t + 1))
                    for k in range(KC):
                        last = pe.matmul(work_tiles[:, t, 0:width], turned[:, k, tile], weight[:, k, 0:width],
                                         start=(k == 0), stop=(k == KC - 1))
                return last

            def project_out(m, i, n):
                rows(weights["b_o" if causal(m) else "a_o"], i, D, "x_ready").then_inc(on["added_full"], 1)

            def gates(m, i, n):
                rows(gate_w, i, NODES, "gates").then_inc(on["gates_full"], 1)

            def mix(m, i, n):
                rows(leaf_w, i, D, "x_ready").then_inc(on["added_full"], 1)

            def values(m, i, n):
                rows(weights["b_v" if causal(m) else "a_v"], i, D, "values_ready").then_inc(on["values_full"], 1)

            def heads(which):
                def step(m, i, n):
                    weight = weights[("b_" if causal(m) else "a_") + which]
                    pe.wait_ge(on["turned"], count.of("turned"))
                    take_work("raw_ready" if causal(m) else "rest")
                    for k in range(KC):
                        last = pe.matmul(ps_work[:, :], weight[:, k, P * i:P * i + P], turned[:, k, :],
                                         start=(k == 0), stop=(k == KC - 1))
                    last.then_inc(on["heads_full"], 1)
                return step

            def rotate(m, i, n):
                if causal(m):
                    count.add("rest", 2)

            program(pe, count, core, dict(turn_attended=turn_attended, turn_normed=turn_normed,
                                          turn_leaves=turn_leaves, project_out=project_out, gates=gates, mix=mix,
                                          values=values, heads_k=heads("k"), heads_q=heads("q"), rotate_k=rotate,
                                          rotate_q=rotate), opening, closing)


def by_pairs(weight):
    inner = weight.shape[1:]
    return np.moveaxis(weight.reshape((HEADS, PAIRS, 2) + inner), (0, 1, 2), (2, 1, 0)).reshape((D,) + inner)


def rope_tables():
    rates = np.float32(THETA) ** (-(np.float32(2.0) * np.arange(PAIRS, dtype=np.float32)) / np.float32(DH))
    angles = np.repeat(rates.astype(np.float32), HEADS)[:, None] * np.arange(T, dtype=np.float32)[None, :]
    return np.cos(angles).astype(np.float32), np.sin(angles).astype(np.float32)


def kernel(**inputs):
    import concourse.bacc as bacc
    from concourse.bass_utils import run_bass_kernel_spmd

    a = {name[3:]: np.asarray(value) for name, value in inputs.items()}
    qkv, qkv_b = a["attn_a_qkv_w"], a["attn_a_qkv_b"]
    cos, sin = rope_tables()
    arrays = dict(
        x=a["attn_a_x"],
        a_q=by_pairs(qkv[:D]).T, a_k=by_pairs(qkv[D:2 * D]).T, a_v=qkv[2 * D:].T, a_o=a["attn_a_out_w"].T,
        a_q_bias=by_pairs(qkv_b[:D]).reshape(2, P).T, a_k_bias=by_pairs(qkv_b[D:2 * D]).reshape(2, P).T,
        a_v_bias=qkv_b[2 * D:], a_o_bias=a["attn_a_out_b"],
        b_q=by_pairs(a["attn_b_Wq"]).T, b_k=by_pairs(a["attn_b_Wk"]).T, b_v=a["attn_b_Wv"].T, b_o=a["attn_b_Wo"].T,
        ffn_q=a["ffn_Wq"], routers=a["ffn_routers"].T, leaf_values=a["ffn_leaf_values"].T, ffn_o=a["ffn_Wout_w"].T,
        ffn_bias=a["ffn_Wout_b"], cosine=cos, sine=sin,
    )
    arrays = {f"in_{name}": np.ascontiguousarray(value) for name, value in arrays.items()}
    nc = bacc.Bacc("TRN2", target_bir_lowering=False, num_devices=1)
    w = {n[3:]: nc.dram_tensor(n, v.shape, F32, kind="ExternalInput").ap() for n, v in arrays.items()}
    out = nc.dram_tensor("out", (BATCH, T, D), F32, kind="ExternalOutput").ap()
    build(nc, w.pop("x"), w, out)
    return run_bass_kernel_spmd(nc, [arrays], core_ids=[0]).results[0]["out"]
```

```python
from contextlib import ExitStack

import numpy as np

import concourse.bass as bass
from concourse import mybir

F32 = mybir.dt.float32
BF16 = mybir.dt.bfloat16
ALU = mybir.AluOpType
ACT = mybir.ActivationFunctionType
AX_X = mybir.AxisListType.X

P = 128
BATCH, T, D = 8, 512, 256
HEADS = 16
DH = D // HEADS
PAIRS = DH // 2
TILES = T // P
KC = D // P
LEVELS = 8
LEAVES = 2 ** LEVELS
NODES = LEAVES - 1
EPS = 1e-5
THETA = 10000.0
SCALE = float(DH) ** -0.5
MASKED = -1e30
DMA = 16

GROUP = 4
GROUPS = HEADS // GROUP
COLS = 32
VALUE = DH + 1

QUERY_PARTS = (0, 0, 0, 1, 1, 2)
KEY_PARTS = (0, 1, 2, 0, 1, 0)
SPLIT_ROWS = len(QUERY_PARTS) * DH
SHIFT_ROW = SPLIT_ROWS
STACK_ROWS = SPLIT_ROWS + 1
STACK_DMAS = 2 * 2 * len(QUERY_PARTS)

STEPS = GROUPS * TILES
SLOTS = STEPS * GROUP
GROUP_SLOTS = SLOTS // GROUPS
LEAD = 28
SHIFT_LAG = 6
MIX_LAG = 8
OUT_LAG = MIX_LAG + 1
TURN_LAG = MIX_LAG + 3
RING = 4
SCORE_BANKS = 3

PHASES = 2 * BATCH
AHEAD = 3
LOOP_FIRST, LOOP_PHASES = AHEAD, 2
TURNS = BATCH - AHEAD

FINISH = (
    (1, "bias_input", 0), (3, "bias_input", 1), (10, "turn_attended", 0), (12, "turn_attended", 1),
    (14, "project_out", 0), (16, "project_out", 1), (24, "moments", 0), (25, "moments", 1), (26, "spread", 0),
    (29, "normalize", 0), (30, "normalize", 1), (32, "turn_normed", 0), (33, "bias_stream", 0),
    (34, "turn_normed", 1), (35, "bias_stream", 1), (37, "gates", 0), (40, "gates", 1), (42, "leaves", 0),
    (43, "leaves", 1), (44, "leaves", 2), (45, "leaves", 3), (46, "leaves", 4), (48, "turn_leaves", 0),
    (50, "turn_leaves", 1), (54, "mix", 0), (58, "mix", 1),
)
PREPARE = (
    (3, "moments", 0), (4, "moments", 1), (5, "spread", 0), (7, "normalize", 0), (8, "normalize", 1),
    (9, "turn_normed", 0), (11, "turn_normed", 1),
    (13, "heads_k", 0), (14, "products_k", 0), (15, "heads_k", 1), (15, "products_k", 1), (16, "products_k", 2),
    (17, "heads_q", 0), (17, "products_k", 3), (18, "rotate_k", 0), (19, "heads_q", 1), (19, "rotate_k", 1),
    (19, "high_k", 0), (20, "products_q", 0), (20, "high_k", 1), (20, "rest_k", 0), (21, "products_q", 1),
    (21, "rest_k", 1), (22, "products_q", 2), (22, "middle_k", 0), (23, "products_q", 3),
    (23, "middle_k", 1), (24, "low_k", 0), (24, "rotate_q", 0), (25, "low_k", 1), (25, "rotate_q", 1),
    (25, "high_q", 0), (26, "high_q", 1), (27, "rest_q", 0), (28, "rest_q", 1), (28, "middle_q", 0),
    (28, "values", 0), (29, "middle_q", 1), (29, "low_q", 0), (30, "low_q", 1), (30, "values", 1),
)
LEAF_LEVELS = ((0, 1, 2, 3), (4, 5), (6,), (7,), (7,))

PER_TURN = dict(
    scores_full=2 * 64, max_done=2 * 64, shift_full=2 * 4, shift_row=2 * 4, shift_sent0=2 * 2, shift_sent1=2 * 2,
    keyed_full=2 * 64, exp_done=2 * 64, causal_done=16, mixed_done=2 * 16, out_ready=2 * 4,
    out_turned=2 * 4, inverse_done=2 * 4, attended=2 * 4,
    moments_done=2 * 4, spread_done=2 * 2, variance=2 * 2, rstd=2 * 2, normed=2 * 4, turned_full=2 * 8,
    turned=2 * 8, added_full=2 * 4, x_ready=2 * 4, biased=2 * 3, gates_full=2 * 2, gates=2 * 2, level_done=2 * 9,
    heads_full=2 * 4, raw_ready=2 * 4, product_done=8, rotated=4, high=2 * 4, rest=2 * 4, middle=2 * 4, low=2 * 4,
    values_full=2 * 2, values_ready=2 * 2,
    stacked0=STACK_DMAS, stacked1=STACK_DMAS, x_loaded=1, x_again=1, moved=1, kept=1, stored=1,
)


def causal(n):
    return n >= PHASES - AHEAD or (n >= AHEAD and n % 2 == AHEAD % 2)


def element(n):
    if n >= PHASES - AHEAD:
        return n - PHASES + BATCH
    return n if n < AHEAD else (n - AHEAD) // 2 + (0 if causal(n) else AHEAD)


def schedule(n):
    due = {}
    if n > 0:
        for slot, step, i in FINISH:
            due.setdefault(slot, []).append((step, i, n - 1))
    if n + 1 < PHASES:
        for slot, step, i in PREPARE:
            due.setdefault(slot, []).append((step, i, n + 1))
    return due


def score_unit(n, slot):
    n, unit = n + (slot + LEAD) // SLOTS, (slot + LEAD) % SLOTS
    return n, unit, unit // 16, unit % 16 // TILES, unit % TILES


def shift_due(n, unit):
    return unit % 16 == SHIFT_LAG and 16 < n * SLOTS + unit < PHASES * SLOTS + 16


class Count:

    def __init__(self):
        self.n = dict.fromkeys(PER_TURN, 0)
        self.turn = None

    def add(self, event, times=1):
        self.n[event] += times

    def some(self, event, back=0):
        return self.turn is not None or self.n[event] > back

    def of(self, event, back=0):
        n = self.n[event] - back
        return n if self.turn is None else self.turn * PER_TURN[event] + n

    def next(self, event):
        self.add(event)
        return self.of(event)

    def enter(self, turn):
        self.turn, self.start = turn, dict(self.n)

    def leave(self):
        self.turn = None
        for event, n in self.n.items():
            grown = n - self.start[event]
            assert grown in (0, PER_TURN[event]), (event, grown, PER_TURN[event])
            self.n[event] += grown * (TURNS - 1)


def build(nc, x, w, out):
    with ExitStack() as ctx:
        def sb(name, shape, dt=F32):
            return ctx.enter_context(nc.sbuf_tensor(name, shape, dt))

        def bank(name, shape):
            return ctx.enter_context(nc.psum_tensor(name, shape, F32))

        def sem(name):
            return ctx.enter_context(nc.semaphore(name))

        weights = {k: sb(k, [P, KC, D]) for k in ("a_q", "a_k", "a_v", "a_o", "b_q", "b_k", "b_v", "b_o")}
        gate_w = sb("gate_w", [P, KC, D])
        leaf_w = sb("leaf_w", [P, KC, D])
        head_bias = {k: sb(k, [P, 2]) for k in ("a_q_bias", "a_k_bias")}
        wide_bias = {k: sb(k, [P, D]) for k in ("a_v_bias", "a_o_bias", "ffn_bias")}
        cosine = sb("cosine", [P, T])
        sine = sb("sine", [P, T])
        ident = sb("ident", [P, P])
        ident_b = sb("ident_b", [P, P], BF16)
        mask_b = sb("mask_b", [P, P], BF16)
        minus_half = sb("minus_half", [P, TILES])

        x_in = sb("x_in", [P, TILES, D])
        x_again = sb("x_again", [P, TILES, D])
        x_plain = sb("x_plain", [P, TILES, D])
        x_moved = sb("x_moved", [P, TILES, D])
        x_kept = sb("x_kept", [P, TILES, D])
        x_causal = sb("x_causal", [P, TILES, D])

        q_stack = [sb(f"q_stack{s}", [P, HEADS, T], BF16) for s in range(2)]
        k_stack = [sb(f"k_stack{s}", [P, HEADS, T], BF16) for s in range(2)]
        v_flat = [sb(f"v_ones{s}", [P, TILES * HEADS * VALUE + COLS - VALUE]) for s in range(2)]

        def values_of(s):
            return v_flat[s][:, 0:TILES * HEADS * VALUE].rearrange("p (t h d) -> p t h d", t=TILES, h=HEADS)

        turned_heads = sb("turned_heads", [P, KC, T])
        turned_block = sb("turned_block", [P, KC, T])
        attended = sb("attended", [P, TILES, D])
        parts = {k: [sb(f"{k}_part{i}", [P, 2, T], BF16) for i in range(3)] for k in "qk"}
        scratch = sb("scratch", [P, 5, 1024])
        probs = [sb(f"probs{i}", [P, GROUP, T]) for i in range(RING)]
        out_raw = [sb(f"out_raw{i}", [P, T]) for i in range(2)]
        neg_max = [sb(f"neg_max{i}", [P, TILES, GROUP], BF16) for i in range(2)]
        shift_rows = [sb(f"shift_rows{i}", [GROUP, T], BF16) for i in range(2)]
        inverse = sb("inverse", [P, TILES, GROUP])
        moments = sb("moments", [P, TILES, 6])
        spread = sb("spread", [P, TILES, 2])
        variance = sb("variance", [P, TILES])
        rstd = sb("rstd", [P, TILES])

        def tiles_of(i):
            return scratch[:, i, :].rearrange("p (t n) -> p t n", t=TILES)

        def halves_of(i):
            return scratch[:, i, :].rearrange("p (c n) -> p c n", c=2)

        def staged(i, n):
            return scratch[:, 1 + i // 2, 512 * (i % 2):512 * (i % 2) + KC * n].rearrange("p (k n) -> p k n", k=KC)

        normed_block, tanh_gates, leaf_probs = tiles_of(0), tiles_of(0), [tiles_of(1), tiles_of(2)]
        raw = dict(k=halves_of(0), q=halves_of(3))
        by_cos, by_sin = halves_of(1), halves_of(2)
        normed_heads, rest = tiles_of(4), halves_of(4)

        ps_max = [bank(f"ps_max{i}", [P, T]) for i in range(SCORE_BANKS)]
        ps_key = [bank(f"ps_key{i}", [P, T]) for i in range(2)]
        ps_out = bank("ps_out", [P, T])
        ps_turn = bank("ps_turn", [P, T])
        ps_work = bank("ps_work", [P, T])
        work_tiles = ps_work[:, :].rearrange("p (t n) -> p t n", t=2)
        turn_heads = ps_turn[:, :].rearrange("p (q j c) -> p q j c", q=TILES, j=GROUP)
        turn_shift = ps_turn[0:GROUP, 0:T // 2].bitcast(BF16)

        on = {name: sem(name) for name in PER_TURN}
        first_loaded = sem("first_loaded")
        rest_loaded = sem("rest_loaded")
        zeroed = sem("zeroed")
        constants = sem("constants")
        ones_set = sem("ones_set")
        fold_full = sem("fold_full")
        folded = sem("folded")
        FIRST = ("a_k", "a_q", "a_v", "a_k_bias", "a_q_bias", "a_v_bias")
        REST = ("a_o", "b_q", "b_k", "b_v", "b_o", "a_o_bias", "ffn_bias", "cosine", "sine",
                "ffn_q", "routers", "leaf_values", "ffn_o")
        block = ctx.enter_context(nc.Block())

        def load_weight(eng, name, loaded):
            by_rows = lambda ap: ap.rearrange("(k p) n -> p k n", p=P)
            if name in weights:
                dst, src = weights[name][:, :, :], by_rows(w[name])
            elif name in head_bias:
                dst, src = head_bias[name][:, :], w[name]
            elif name in wide_bias:
                dst, src = wide_bias[name][:, :], w[name].partition_broadcast(P)
            elif name in ("cosine", "sine"):
                dst, src = (cosine if name == "cosine" else sine)[:, :], w[name]
            else:
                at = ("ffn_q", "routers", "leaf_values", "ffn_o").index(name)
                dst, src = staged(at, w[name].shape[1]), by_rows(w[name])
            eng.dma_start(dst, src).then_inc(loaded, DMA)

        def program(eng, count, core, steps, opening, closing):
            def phase(n):
                due = schedule(n)
                for slot in range(SLOTS):
                    core(n, slot)
                    for step, i, m in due.get(slot, ()):
                        if step in steps:
                            steps[step](m, i, n)

            for _, step, i in PREPARE:
                if step in steps:
                    steps[step](0, i, -1)
            opening()
            for n in range(LOOP_FIRST):
                phase(n)
            with eng.Fori(0, TURNS) as turn:
                count.enter(turn)
                for n in range(LOOP_FIRST, LOOP_FIRST + LOOP_PHASES):
                    phase(n)
            count.leave()
            for n in range(LOOP_FIRST + TURNS * LOOP_PHASES, PHASES):
                phase(n)
            closing()
            for _, step, i in FINISH:
                if step in steps:
                    steps[step](PHASES - 1, i, PHASES)

        def stream(m, n):
            if n >= m:
                return x_causal if causal(m) else x_plain
            return x_in if not causal(m) else x_moved if m < PHASES - 1 else x_plain

        def kept(m):
            return x_kept if m < PHASES - 2 else x_moved if m < PHASES - 1 else x_plain

        @block.sync
        def _(sp):
            count = Count()

            def one(tensor, e):
                got = tensor[e] if count.turn is None else tensor[bass.ds(count.turn + e, 1)].squeeze(0)
                return got.rearrange("(t p) d -> p t d", p=P)

            def load_x(m):
                if count.some("normed"):
                    sp.wait_ge(on["normed"], count.of("normed"))
                    sp.nop(nofuse=True)
                sp.dma_start(x_in[:, :, :], one(x, element(m))).then_inc(on["x_loaded"], DMA)

            def load_again(m):
                if count.some("x_ready"):
                    sp.wait_ge(on["x_ready"], count.of("x_ready"))
                    sp.nop(nofuse=True)
                sp.dma_start(x_again[:, :, :], one(x, element(m))).then_inc(on["x_again"], DMA)

            def core(n, slot):
                if slot == 0:
                    if n > 0:
                        count.add("keyed_full", SLOTS)
                    if n + 1 < PHASES and not causal(n + 1):
                        load_x(n + 1)
                if slot == 40 and not causal(n):
                    load_again(n)

            def stack(m, which, part):
                dst = (q_stack if which == "q" else k_stack)[m % 2]
                held = on["stacked0"] if m % 2 == 0 else on["stacked1"]
                for c in range(2):
                    for r, holds in enumerate(QUERY_PARTS if which == "q" else KEY_PARTS):
                        if holds == part:
                            row = DH * r + PAIRS * c
                            sp.dma_start(dst[row:row + PAIRS, :, :], parts[which][part][:, c, :]).then_inc(held, DMA)

            def stack_high(which):
                def step(m, i, n):
                    count.add("high")
                    if i == 0:
                        return
                    if count.some("keyed_full"):
                        sp.wait_ge(on["keyed_full"], count.of("keyed_full"))
                        sp.nop(nofuse=True)
                    sp.wait_ge(on["high"], count.of("high"))
                    sp.nop(nofuse=True)
                    stack(m, which, 0)
                return step

            def stack_middle(which):
                def step(m, i, n):
                    count.add("middle")
                    if i == 1:
                        sp.wait_ge(on["middle"], count.of("middle"))
                        sp.nop(nofuse=True)
                        stack(m, which, 1)
                return step

            def stack_low(which):
                def step(m, i, n):
                    count.add("low")
                    if i == 1:
                        sp.wait_ge(on["low"], count.of("low"))
                        sp.nop(nofuse=True)
                        stack(m, which, 2)
                return step

            def normalize(m, i, n):
                count.add("normed")

            def move():
                sp.wait_ge(on["x_ready"], count.of("x_ready"))
                sp.nop(nofuse=True)
                sp.wait_ge(on["normed"], count.of("normed"))
                sp.nop(nofuse=True)
                if count.some("kept"):
                    sp.wait_ge(on["kept"], count.of("kept") * DMA)
                    sp.nop(nofuse=True)
                sp.dma_start(x_moved[:, :, :], x_plain[:, :, :]).then_inc(on["moved"], DMA)
                count.add("moved")

            def keep():
                sp.wait_ge(on["x_ready"], count.of("x_ready"))
                sp.nop(nofuse=True)
                sp.wait_ge(on["moved"], count.of("moved") * DMA)
                sp.nop(nofuse=True)
                sp.dma_start(x_kept[:, :, :], x_moved[:, :, :]).then_inc(on["kept"], DMA)
                count.add("kept")

            def project_out(m, i, n):
                count.add("x_ready")
                if i == 1 and causal(m) and n < PHASES - AHEAD:
                    keep()
                    move()

            def mix(m, i, n):
                count.add("x_ready")
                if i == 1 and m == 1:
                    keep()
                if i == 1 and m < 2:
                    move()
                if i == 1 and causal(m):
                    sp.wait_ge(on["x_ready"], count.of("x_ready"))
                    sp.nop(nofuse=True)
                    sp.dma_start(one(out, element(m)), x_causal[:, :, :]).then_inc(on["stored"], DMA)
                    count.add("stored")

            def opening():
                pass

            sp.sem_inc(on["stored"], DMA)
            count.add("stored")
            load_x(0)
            for name in FIRST:
                load_weight(sp, name, first_loaded)
            program(sp, count, core, dict(high_k=stack_high("k"), middle_k=stack_middle("k"),
                                          low_k=stack_low("k"), high_q=stack_high("q"),
                                          middle_q=stack_middle("q"), low_q=stack_low("q"),
                                          normalize=normalize, project_out=project_out, mix=mix),
                    opening, opening)
            sp.wait_ge(on["stored"], count.of("stored") * DMA)

        @block.gpsimd
        def _(pool):
            count = Count()
            for t in (ident, ident_b, mask_b):
                pool.memset(t[:, :], 0.0).then_inc(zeroed, 1)
            pool.memset(minus_half[:, :], -0.5).then_inc(zeroed, 1)
            for s in range(2):
                pool.memset(v_flat[s][:, TILES * HEADS * VALUE:], 0.0).then_inc(zeroed, 1)
                pool.memset(values_of(s)[:, :, :, DH:VALUE], 1.0).then_inc(constants, 1)
            pool.wait_ge(zeroed, 6)
            for t in (ident, ident_b):
                pool.affine_select(out=t[:, :], in_=t[:, :], compare_op=ALU.not_equal, fill=1.0, base=0,
                                   pattern=[[-1, P]], channel_multiplier=1).then_inc(constants, 1)
            pool.affine_select(out=mask_b[:, :], in_=mask_b[:, :], compare_op=ALU.is_ge, fill=MASKED, base=0,
                               pattern=[[-1, P]], channel_multiplier=1).then_inc(constants, 1)

            def send_shift(n, slot):
                n, unit, g, _, _ = score_unit(n, slot)
                if not shift_due(n, unit):
                    return
                n, g = (n, g - 1) if g else (n - 1, GROUPS - 1)
                pool.wait_ge(on["shift_row"], count.next("shift_row"))
                pool.nop(nofuse=True)
                sent = on["shift_sent0"] if g % 2 == 0 else on["shift_sent1"]
                pool.dma_start(q_stack[n % 2][SHIFT_ROW:STACK_ROWS, GROUP * g:GROUP * (g + 1), :],
                               shift_rows[g % 2][:, :]).then_inc(sent, DMA)

            def core(n, slot):
                send_shift(n, slot)
                step, r = slot // 4, slot % 4
                if r == 3:
                    count.add("exp_done", GROUP)
                    if causal(n):
                        kb = step % TILES
                        tile = probs[step % RING][:, :, P * kb:P * kb + P]
                        pool.wait_ge(on["exp_done"], count.of("exp_done"))
                        pool.nop(nofuse=True)
                        pool.affine_select(out=tile, in_=tile, compare_op=ALU.is_ge, fill=0.0, base=0,
                                           pattern=[[0, GROUP], [1, P]], channel_multiplier=-1)\
                            .then_inc(on["causal_done"], 1)

            def add_bias(dst, i, bias):
                two = dst[:, 2 * i:2 * i + 2, :]
                row = wide_bias[bias][:, :].unsqueeze(1).broadcast_to([P, 2, D])
                pool.tensor_tensor(two, two, row, ALU.add).then_inc(on["biased"], 1)

            def bias_input(m, i, n):
                if not causal(m):
                    if i == 0:
                        pool.wait_ge(on["x_again"], count.next("x_again") * DMA)
                        pool.nop(nofuse=True)
                    add_bias(x_again, i, "a_o_bias")

            def spread_step(m, i, n):
                pool.wait_ge(on["variance"], count.next("variance"))
                pool.nop(nofuse=True)
                pool.tensor_tensor(rstd[:, :], variance[:, :], minus_half[:, :], ALU.pow).then_inc(on["rstd"], 1)

            def normalize(m, i, n):
                count.add("normed")

            def bias_stream(m, i, n):
                if i == 0:
                    pool.wait_ge(on["normed"], count.of("normed"))
                    pool.nop(nofuse=True)
                add_bias(stream(m, n), i, "ffn_bias")

            def products(which):
                def step(m, i, n):
                    if not causal(m):
                        return
                    c = i // 2
                    if i % 2 == 0:
                        pool.wait_ge(on["raw_ready"], count.next("raw_ready"))
                        pool.nop(nofuse=True)
                    if i == 0 and count.some("rotated"):
                        pool.wait_ge(on["rotated"], count.of("rotated"))
                        pool.nop(nofuse=True)
                    dst, factor = (by_sin, sine) if i % 2 else (by_cos, cosine)
                    pool.tensor_tensor(dst[:, c, :], raw[which][:, c, :], factor[:, :], ALU.mult)\
                        .then_inc(on["product_done"], 1)
                return step

            def heads(m, i, n):
                if not causal(m):
                    count.add("raw_ready")

            def rotate(m, i, n):
                if causal(m):
                    count.add("rotated")

            def low_part(which):
                def step(m, i, n):
                    pool.wait_ge(on["middle"], count.next("middle"))
                    pool.nop(nofuse=True)
                    pool.tensor_tensor(parts[which][2][:, i, :], rest[:, i, :], parts[which][1][:, i, :],
                                       ALU.subtract).then_inc(on["low"], 1)
                return step

            def opening():
                pool.wait_ge(rest_loaded, DMA * len(REST))
                for slot in range(-LEAD, 0):
                    send_shift(0, slot)

            def closing():
                pass

            program(pool, count, core, dict(bias_input=bias_input, spread=spread_step, normalize=normalize,
                                            bias_stream=bias_stream, heads_k=heads, heads_q=heads,
                                            products_k=products("k"), products_q=products("q"),
                                            rotate_k=rotate, rotate_q=rotate, low_k=low_part("k"),
                                            low_q=low_part("q")), opening, closing)

        @block.scalar
        def _(act):
            count = Count()
            for name in REST:
                load_weight(act, name, rest_loaded)
            act.wait_ge(first_loaded, DMA * len(FIRST))

            def core(n, slot):
                step, j = slot // GROUP, slot % GROUP
                kb = step % TILES
                q0 = P * kb if causal(n) else 0
                if j == 0:
                    if count.some("mixed_done", RING - 1):
                        act.wait_ge(on["mixed_done"], count.of("mixed_done", RING - 1))
                    count.add("mixed_done")
                act.wait_ge(on["keyed_full"], count.next("keyed_full"))
                act.activation(probs[step % RING][:, j, q0:T], ps_key[slot % 2][:, 0:T - q0], ACT.Exp,
                               scale=SCALE).then_inc(on["exp_done"], 1)
                if slot % GROUP_SLOTS == (GROUP_SLOTS - GROUP + OUT_LAG) % GROUP_SLOTS and (n > 0 or slot >= GROUP_SLOTS):
                    copy_out((slot // GROUP_SLOTS - 1) % GROUPS, OUT_LAG // GROUP)

            def copy_out(g, begun):
                act.wait_ge(on["mixed_done"], count.of("mixed_done", begun))
                act.activation(out_raw[g % 2][:, :], ps_out[:, :], ACT.Copy).then_inc(on["out_ready"], 1)

            def opening():
                pass

            def closing():
                copy_out(GROUPS - 1, 0)

            def turn(m, i, n):
                act.wait_ge(on["turned_full"], count.next("turned_full"))
                dst = turned_heads if n < m else turned_block
                act.activation(dst[:, i, :], ps_work[:, :], ACT.Copy).then_inc(on["turned"], 1)

            def gates(m, i, n):
                act.wait_ge(on["gates_full"], count.next("gates_full"))
                act.activation(tanh_gates[:, 2 * i:2 * i + 2, 0:NODES], work_tiles[:, :, 0:NODES], ACT.Tanh,
                               scale=0.5).then_inc(on["gates"], 1)

            def heads(which):
                def step(m, i, n):
                    act.wait_ge(on["heads_full"], count.next("heads_full"))
                    dst = raw[which][:, i, :]
                    if causal(m):
                        act.activation(dst, ps_work[:, :], ACT.Copy).then_inc(on["raw_ready"], 1)
                    else:
                        act.activation(dst, ps_work[:, :], ACT.Identity,
                                       bias=head_bias[f"a_{which}_bias"][:, i:i + 1]).then_inc(on["raw_ready"], 1)
                    count.add("raw_ready")
                return step

            def high_part(which):
                def step(m, i, n):
                    if causal(m):
                        act.wait_ge(on["rotated"], count.next("rotated"))
                    else:
                        act.wait_ge(on["raw_ready"], count.of("raw_ready"))
                    act.activation(parts[which][0][:, i, :], raw[which][:, i, :], ACT.Copy).then_inc(on["high"], 1)
                return step

            def middle_part(which):
                def step(m, i, n):
                    act.wait_ge(on["rest"], count.next("rest"))
                    act.activation(parts[which][1][:, i, :], rest[:, i, :], ACT.Copy).then_inc(on["middle"], 1)
                return step

            def values(m, i, n):
                count.add("values_full")
                if causal(m):
                    act.wait_ge(on["values_full"], count.of("values_full"))
                    act.activation(values_of(m % 2)[:, 2 * i:2 * i + 2, :, 0:DH],
                                   work_tiles.rearrange("p t (h d) -> p t h d", h=HEADS), ACT.Copy)\
                       .then_inc(on["values_ready"], 1)

            program(act, count, core, dict(turn_attended=turn, turn_normed=turn, turn_leaves=turn, gates=gates,
                                           heads_k=heads("k"), heads_q=heads("q"), high_k=high_part("k"),
                                           high_q=high_part("q"), middle_k=middle_part("k"),
                                           middle_q=middle_part("q"), values=values), opening, closing)

        @block.vector
        def _(dve):
            count = Count()
            for s in range(2):
                dve.memset(k_stack[s][SHIFT_ROW:STACK_ROWS, :, :], 1.0).then_inc(ones_set, 1)
            dve.wait_ge(first_loaded, DMA * len(FIRST))

            def largest(n, slot):
                n, unit, g, j, qt = score_unit(n, slot)
                if n < PHASES:
                    keys = P * (qt + 1) if causal(n) else T
                    dve.wait_ge(on["scores_full"], count.next("scores_full"))
                    dve.tensor_reduce(out=neg_max[g % 2][:, qt, j:j + 1], in_=ps_max[unit % SCORE_BANKS][:, 0:keys],
                                      axis=AX_X, op=ALU.max, negate=True).then_inc(on["max_done"], 1)
                if shift_due(n, unit):
                    h = (g + 1) % 2
                    sent = on["shift_sent0"] if h == 0 else on["shift_sent1"]
                    dve.wait_ge(on["shift_full"], count.next("shift_full"))
                    if count.some(f"shift_sent{h}"):
                        dve.wait_ge(sent, count.of(f"shift_sent{h}") * DMA)
                    count.add(f"shift_sent{h}")
                    dve.tensor_copy(shift_rows[h][:, :], turn_shift).then_inc(on["shift_row"], 1)

            def divide(g):
                dve.wait_ge(on["out_turned"], count.next("out_turned"))
                dve.reciprocal(inverse[:, :, :], turn_heads[:, :, :, DH]).then_inc(on["inverse_done"], 1)
                dve.wait_ge(on["inverse_done"], count.next("inverse_done"))
                dst = attended[:, :, GROUP * DH * g:GROUP * DH * (g + 1)].rearrange("p q (j d) -> p q j d", j=GROUP)
                dve.tensor_tensor(dst, turn_heads[:, :, :, 0:DH],
                                  inverse[:, :, :].unsqueeze(3).broadcast_to([P, TILES, GROUP, DH]), ALU.mult)\
                   .then_inc(on["attended"], 1)

            def core(n, slot):
                largest(n, slot)
                if slot % GROUP_SLOTS == (GROUP_SLOTS - GROUP + TURN_LAG) % GROUP_SLOTS and (n > 0 or slot >= GROUP_SLOTS):
                    divide((slot // GROUP_SLOTS - 1) % GROUPS)

            def opening():
                dve.wait_ge(rest_loaded, DMA * len(REST))
                dve.wait_ge(fold_full, 1)
                for c in range(KC):
                    dve.tensor_copy(gate_w[:, c, 0:NODES], ps_max[c][:, 0:NODES]).then_inc(folded, 1)
                    dve.tensor_scalar(leaf_w[:, c, :], ps_key[c][:, 0:D], 2.0 ** -LEVELS, None, ALU.mult)\
                       .then_inc(folded, 1)
                for slot in range(-LEAD, 0):
                    largest(0, slot)

            def closing():
                divide(GROUPS - 1)

            def add(m, i, n, src):
                two = slice(2 * i, 2 * i + 2)
                dst = x_causal if causal(m) else x_plain
                dve.wait_ge(on["added_full"], count.next("added_full"))
                dve.tensor_tensor(dst[:, two, :], work_tiles, src[:, two, :], ALU.add).then_inc(on["x_ready"], 1)
                count.add("x_ready")

            def project_out(m, i, n):
                if i == 0 and causal(m):
                    dve.wait_ge(on["kept"], count.of("kept") * DMA)
                    dve.wait_ge(on["stored"], count.next("stored") * DMA)
                elif i == 0:
                    count.add("biased", 2)
                    dve.wait_ge(on["biased"], count.of("biased"))
                    if count.some("moved"):
                        dve.wait_ge(on["moved"], count.of("moved") * DMA)
                add(m, i, n, kept(m) if causal(m) else x_again)
                if i == 1 and causal(m) and n < PHASES - AHEAD:
                    count.add("kept")
                    count.add("moved")

            def mix(m, i, n):
                if i == 0:
                    count.add("biased", 2)
                    dve.wait_ge(on["biased"], count.of("biased"))
                add(m, i, n, stream(m, n))
                if i == 1 and m < 2:
                    count.add("moved")
                    count.add("kept", m)

            def moments_step(m, i, n):
                src = stream(m, n)
                if i == 1:
                    pass
                elif src is x_in:
                    dve.wait_ge(on["x_loaded"], count.next("x_loaded") * DMA)
                elif src is x_moved:
                    dve.wait_ge(on["moved"], count.of("moved") * DMA)
                else:
                    dve.wait_ge(on["x_ready"], count.of("x_ready"))
                for t in (2 * i, 2 * i + 1):
                    last = dve.bn_stats(moments[:, t, :], src[:, t, :])
                last.then_inc(on["moments_done"], 1)
                count.add("moments_done")

            def spread_step(m, i, n):
                dve.wait_ge(on["moments_done"], count.of("moments_done"))
                dve.nop(nofuse=True)
                for t in range(TILES):
                    last = dve.bn_aggr(spread[:, t, :], moments[:, t, :])
                last.then_inc(on["spread_done"], 1)
                dve.wait_ge(on["spread_done"], count.next("spread_done"))
                dve.tensor_scalar(variance[:, :], spread[:, :, 1], EPS, None, ALU.add).then_inc(on["variance"], 1)

            def normalize(m, i, n):
                src = stream(m, n)
                if i == 0:
                    dve.wait_ge(on["rstd"], count.next("rstd"))
                    if n < m and count.some("low"):
                        dve.wait_ge(on["low"], count.of("low"))
                dst = normed_heads if n < m else normed_block
                for t in (2 * i, 2 * i + 1):
                    last = dve.tensor_scalar(dst[:, t, :], src[:, t, :], spread[:, t, 0:1], rstd[:, t:t + 1],
                                             ALU.subtract, ALU.mult)
                last.then_inc(on["normed"], 1)

            def leaves(m, i, n):
                if i == 0:
                    count.add("gates", 2)
                    dve.wait_ge(on["gates"], count.of("gates"))
                for level in LEAF_LEVELS[i]:
                    nodes = 2 ** level
                    gate = tanh_gates[:, :, nodes - 1:2 * nodes - 1]
                    above = leaf_probs[(level + 1) % 2][:, :, 0:nodes]
                    below = leaf_probs[level % 2][:, :, 0:2 * nodes].rearrange("p t (n s) -> p t n s", s=2)
                    left, right = level < LEVELS - 1 or i == 3, level < LEVELS - 1 or i == 4
                    if level == 0:
                        dve.tensor_scalar(below[:, :, :, 0], gate, -1.0, 1.0, ALU.mult, ALU.add)
                        last = dve.tensor_scalar(below[:, :, :, 1], gate, 1.0, None, ALU.add)
                    else:
                        dve.wait_ge(on["level_done"], count.of("level_done"))
                        if left:
                            last = dve.scalar_tensor_tensor(out=below[:, :, :, 0], in0=gate, scalar=1.0, in1=above,
                                                            op0=ALU.subtract, op1=ALU.mult, reverse0=True)
                        if right:
                            last = dve.scalar_tensor_tensor(out=below[:, :, :, 1], in0=gate, scalar=1.0, in1=above,
                                                            op0=ALU.add, op1=ALU.mult)
                    last.then_inc(on["level_done"], 1)
                    count.add("level_done")

            def rotate(which):
                def step(m, i, n):
                    if not causal(m):
                        return
                    if i == 0:
                        count.add("product_done", 4)
                        dve.wait_ge(on["product_done"], count.of("product_done"))
                        dve.tensor_tensor(raw[which][:, 0, :], by_cos[:, 0, :], by_sin[:, 1, :], ALU.subtract)\
                           .then_inc(on["rotated"], 1)
                    else:
                        dve.tensor_tensor(raw[which][:, 1, :], by_sin[:, 0, :], by_cos[:, 1, :], ALU.add)\
                           .then_inc(on["rotated"], 1)
                return step

            def rest_part(which):
                def step(m, i, n):
                    dve.wait_ge(on["high"], count.next("high"))
                    if i == 0 and which == "q":
                        dve.wait_ge(on["low"], count.of("low"))
                    dve.tensor_tensor(rest[:, i, :], raw[which][:, i, :], parts[which][0][:, i, :], ALU.subtract)\
                       .then_inc(on["rest"], 1)
                return step

            def low_step(m, i, n):
                count.add("low")

            def values(m, i, n):
                dst = values_of(m % 2)[:, 2 * i:2 * i + 2, :, 0:DH]
                src = work_tiles.rearrange("p t (h d) -> p t h d", h=HEADS)
                count.add("values_full")
                if not causal(m):
                    dve.wait_ge(on["values_full"], count.of("values_full"))
                    bias = wide_bias["a_v_bias"][:, :].rearrange("p (h d) -> p h d", h=HEADS).unsqueeze(1)
                    dve.tensor_tensor(dst, src, bias.broadcast_to([P, 2, HEADS, DH]), ALU.add)\
                       .then_inc(on["values_ready"], 1)

            program(dve, count, core, dict(project_out=project_out, mix=mix, moments=moments_step, spread=spread_step,
                                           normalize=normalize, leaves=leaves, rotate_k=rotate("k"),
                                           rotate_q=rotate("q"), rest_k=rest_part("k"), rest_q=rest_part("q"),
                                           low_k=low_step, low_q=low_step, values=values),
                    opening, closing)

        @block.tensor
        def _(pe):
            count = Count()
            turn_read, work_read = [], []

            def take_turn(event):
                for read in turn_read:
                    pe.wait_ge(on[read], count.of(read))
                turn_read[:] = [event]
                count.add(event)

            def take_work(event):
                for read in work_read:
                    pe.wait_ge(on[read], count.of(read))
                work_read[:] = [event]
                count.add(event)

            pe.wait_ge(constants, 5)
            pe.wait_ge(ones_set, 2)
            pe.wait_ge(first_loaded, DMA * len(FIRST))

            def scores(n, unit, g, j, qt):
                if unit == 0:
                    held = on["stacked0"] if n % 2 == 0 else on["stacked1"]
                    count.add(f"stacked{n % 2}", STACK_DMAS)
                    pe.wait_ge(held, count.of(f"stacked{n % 2}") * DMA)
                h = GROUP * g + j
                keys = P * (qt + 1) if causal(n) else T
                back = 0 if unit == 0 else SCORE_BANKS if unit < SCORE_BANKS else SCORE_BANKS - 1
                if count.some("max_done", back):
                    pe.wait_ge(on["max_done"], count.of("max_done", back))
                count.add("max_done")
                dst = ps_max[unit % SCORE_BANKS]
                last = pe.matmul(dst[:, 0:keys], q_stack[n % 2][0:SPLIT_ROWS, h, P * qt:P * qt + P],
                                 k_stack[n % 2][0:SPLIT_ROWS, h, 0:keys], start=True, stop=not causal(n))
                if causal(n):
                    last = pe.matmul(dst[:, keys - P:keys], ident_b[:, :], mask_b[:, :], start=False, stop=True)
                last.then_inc(on["scores_full"], 1)

            def turn_max(g, begun):
                pe.wait_ge(on["max_done"], count.of("max_done", begun))
                take_turn("shift_row")
                for qt in range(TILES):
                    last = pe.transpose(turn_shift[:, P * qt:P * qt + P], neg_max[g % 2][:, qt, :], ident_b[:, :])
                last.then_inc(on["shift_full"], 1)

            def ahead(n, slot):
                n, unit, g, j, qt = score_unit(n, slot)
                if n < PHASES:
                    scores(n, unit, g, j, qt)
                if shift_due(n, unit):
                    turn_max((g - 1) % GROUPS, SHIFT_LAG + 1 if n < PHASES else 0)

            def by_key(n, slot):
                step, j = slot // GROUP, slot % GROUP
                g, kb = step // TILES, step % TILES
                q0 = P * kb if causal(n) else 0
                if kb == 0 and j == 0:
                    sent = on["shift_sent0"] if g % 2 == 0 else on["shift_sent1"]
                    pe.wait_ge(sent, count.next(f"shift_sent{g % 2}") * DMA)
                if count.some("exp_done", 1):
                    pe.wait_ge(on["exp_done"], count.of("exp_done", 1))
                count.add("exp_done")
                h = GROUP * g + j
                pe.matmul(ps_key[slot % 2][:, 0:T - q0], k_stack[n % 2][0:STACK_ROWS, h, P * kb:P * kb + P],
                          q_stack[n % 2][0:STACK_ROWS, h, q0:T], start=True, stop=True).then_inc(on["keyed_full"], 1)

            def mixed(n, step, begun):
                g, kb = step // TILES, step % TILES
                q0 = P * kb if causal(n) else 0
                if causal(n):
                    pe.wait_ge(on["causal_done"], count.next("causal_done"))
                else:
                    pe.wait_ge(on["exp_done"], count.of("exp_done", begun))
                if step == 0:
                    pe.wait_ge(on["values_ready"], count.of("values_ready"))
                if kb == 0:
                    if count.some("out_ready"):
                        pe.wait_ge(on["out_ready"], count.of("out_ready"))
                    count.add("out_ready")
                for j in range(GROUP):
                    at = VALUE * (HEADS * kb + GROUP * g + j)
                    last = pe.matmul(ps_out[COLS * j:COLS * j + COLS, q0:T], v_flat[n % 2][:, at:at + COLS],
                                     probs[step % RING][:, j, q0:T], start=(kb == 0), stop=(kb == TILES - 1),
                                     tile_position=(0, COLS * j))
                last.then_inc(on["mixed_done"], 1)

            def turn_out(g):
                pe.wait_ge(on["out_ready"], count.of("out_ready"))
                take_turn("attended")
                for qt in range(TILES):
                    last = pe.transpose(ps_turn[:, P * qt:P * qt + P], out_raw[g % 2][:, P * qt:P * qt + P], ident[:, :])
                last.then_inc(on["out_turned"], 1)

            def core(n, slot):
                ahead(n, slot)
                if slot % GROUP_SLOTS == (GROUP_SLOTS - GROUP + TURN_LAG) % GROUP_SLOTS and (n > 0 or slot >= GROUP_SLOTS):
                    turn_out((slot // GROUP_SLOTS - 1) % GROUPS)
                by_key(n, slot)
                if slot % GROUP == MIX_LAG % GROUP:
                    step = (slot - MIX_LAG) // GROUP
                    if step >= 0:
                        mixed(n, step, MIX_LAG - GROUP + 1)
                    elif n > 0:
                        mixed(n - 1, step + STEPS, MIX_LAG - GROUP + 1)

            def opening():
                pe.wait_ge(rest_loaded, DMA * len(REST))
                for c in range(KC):
                    for k in range(KC):
                        pe.matmul(ps_max[c][:, 0:NODES], staged(0, D)[:, k, P * c:P * c + P],
                                  staged(1, NODES)[:, k, :], start=(k == 0), stop=(k == KC - 1))
                for c in range(KC):
                    for k in range(KC):
                        last = pe.matmul(ps_key[c][:, 0:D], staged(2, D)[:, k, P * c:P * c + P],
                                         staged(3, D)[:, k, :], start=(k == 0), stop=(k == KC - 1))
                last.then_inc(fold_full, 1)
                pe.wait_ge(folded, 4)
                for slot in range(-LEAD, 0):
                    ahead(0, slot)

            def closing():
                for late in range(MIX_LAG // GROUP):
                    step = STEPS - MIX_LAG // GROUP + late
                    mixed(PHASES - 1, step, SLOTS - GROUP * (step + 1))
                turn_out(GROUPS - 1)

            def turn_tiles(src, i):
                take_work("turned")
                for t in range(TILES):
                    last = pe.transpose(ps_work[:, P * t:P * t + P], src[:, t, P * i:P * i + P], ident[:, :])
                last.then_inc(on["turned_full"], 1)

            def turn_attended(m, i, n):
                pe.wait_ge(on["attended"], count.of("attended"))
                turn_tiles(attended, i)

            def turn_normed(m, i, n):
                if i == 0:
                    count.add("normed", 2)
                    pe.wait_ge(on["normed"], count.of("normed"))
                turn_tiles(normed_heads if n < m else normed_block, i)

            def turn_leaves(m, i, n):
                if i == 0:
                    count.add("level_done", LEVELS + 1)
                    pe.wait_ge(on["level_done"], count.of("level_done"))
                turn_tiles(leaf_probs[(LEVELS - 1) % 2], i)

            def rows(turned, weight, i, width, read):
                pe.wait_ge(on["turned"], count.of("turned"))
                take_work(read)
                for t in range(2):
                    tile = slice(P * (2 * i + t), P * (2 * i + t + 1))
                    for k in range(KC):
                        last = pe.matmul(work_tiles[:, t, 0:width], turned[:, k, tile], weight[:, k, 0:width],
                                         start=(k == 0), stop=(k == KC - 1))
                return last

            def project_out(m, i, n):
                rows(turned_block, weights["b_o" if causal(m) else "a_o"], i, D, "x_ready").then_inc(on["added_full"], 1)

            def gates(m, i, n):
                rows(turned_block, gate_w, i, NODES, "gates").then_inc(on["gates_full"], 1)

            def mix(m, i, n):
                rows(turned_block, leaf_w, i, D, "x_ready").then_inc(on["added_full"], 1)

            def values(m, i, n):
                rows(turned_heads, weights["b_v" if causal(m) else "a_v"], i, D, "values_ready").then_inc(on["values_full"], 1)

            def heads(which):
                def step(m, i, n):
                    weight = weights[("b_" if causal(m) else "a_") + which]
                    pe.wait_ge(on["turned"], count.of("turned"))
                    take_work("raw_ready")
                    for k in range(KC):
                        last = pe.matmul(ps_work[:, :], weight[:, k, P * i:P * i + P], turned_heads[:, k, :],
                                         start=(k == 0), stop=(k == KC - 1))
                    last.then_inc(on["heads_full"], 1)
                return step

            program(pe, count, core, dict(turn_attended=turn_attended, turn_normed=turn_normed,
                                          turn_leaves=turn_leaves, project_out=project_out, gates=gates, mix=mix,
                                          values=values, heads_k=heads("k"), heads_q=heads("q")),
                    opening, closing)


def by_pairs(weight):
    inner = weight.shape[1:]
    return np.moveaxis(weight.reshape((HEADS, PAIRS, 2) + inner), (0, 1, 2), (2, 1, 0)).reshape((D,) + inner)


def rope_tables():
    rates = np.float32(THETA) ** (-(np.float32(2.0) * np.arange(PAIRS, dtype=np.float32)) / np.float32(DH))
    angles = np.repeat(rates.astype(np.float32), HEADS)[:, None] * np.arange(T, dtype=np.float32)[None, :]
    return np.cos(angles).astype(np.float32), np.sin(angles).astype(np.float32)


def kernel(**inputs):
    import concourse.bacc as bacc
    from concourse.bass_utils import run_bass_kernel_spmd

    a = {name[3:]: np.asarray(value) for name, value in inputs.items()}
    qkv, qkv_b = a["attn_a_qkv_w"], a["attn_a_qkv_b"]
    cos, sin = rope_tables()
    arrays = dict(
        x=a["attn_a_x"],
        a_q=by_pairs(qkv[:D]).T, a_k=by_pairs(qkv[D:2 * D]).T, a_v=qkv[2 * D:].T, a_o=a["attn_a_out_w"].T,
        a_q_bias=by_pairs(qkv_b[:D]).reshape(2, P).T, a_k_bias=by_pairs(qkv_b[D:2 * D]).reshape(2, P).T,
        a_v_bias=qkv_b[2 * D:], a_o_bias=a["attn_a_out_b"],
        b_q=by_pairs(a["attn_b_Wq"]).T, b_k=by_pairs(a["attn_b_Wk"]).T, b_v=a["attn_b_Wv"].T, b_o=a["attn_b_Wo"].T,
        ffn_q=a["ffn_Wq"], routers=a["ffn_routers"].T, leaf_values=a["ffn_leaf_values"].T, ffn_o=a["ffn_Wout_w"].T,
        ffn_bias=a["ffn_Wout_b"], cosine=cos, sine=sin,
    )
    arrays = {f"in_{name}": np.ascontiguousarray(value) for name, value in arrays.items()}
    nc = bacc.Bacc("TRN2", target_bir_lowering=False, num_devices=1)
    w = {n[3:]: nc.dram_tensor(n, v.shape, F32, kind="ExternalInput").ap() for n, v in arrays.items()}
    out = nc.dram_tensor("out", (BATCH, T, D), F32, kind="ExternalOutput").ap()
    build(nc, w.pop("x"), w, out)
    return run_bass_kernel_spmd(nc, [arrays], core_ids=[0]).results[0]["out"]
```

```python
from contextlib import ExitStack

import numpy as np

import concourse.bass as bass
from concourse import mybir

F32 = mybir.dt.float32
BF16 = mybir.dt.bfloat16
ALU = mybir.AluOpType
ACT = mybir.ActivationFunctionType
AX_X = mybir.AxisListType.X

P = 128
BATCH, T, D = 8, 512, 256
HEADS = 16
DH = D // HEADS
PAIRS = DH // 2
TILES = T // P
KC = D // P
LEVELS = 8
LEAVES = 2 ** LEVELS
NODES = LEAVES - 1
EPS = 1e-5
THETA = 10000.0
SCALE = float(DH) ** -0.5
MASKED = -1e30
DMA = 16

GROUP = 4
GROUPS = HEADS // GROUP
COLS = 32
VALUE = DH + 1

QUERY_PARTS = (0, 0, 0, 1, 1, 2)
KEY_PARTS = (0, 1, 2, 0, 1, 0)
SPLIT_ROWS = len(QUERY_PARTS) * DH
SHIFT_ROW = SPLIT_ROWS
STACK_ROWS = SPLIT_ROWS + 1

PLAIN_DMAS = 2 * len(QUERY_PARTS)
CAUSAL_DMAS = 2 * PLAIN_DMAS

STEPS = GROUPS * TILES
SLOTS = STEPS * GROUP
GROUP_SLOTS = SLOTS // GROUPS
LEAD = 24
SHIFT_LAG = 2
MIX_LAG = 8
OUT_LAG = MIX_LAG + 1
TURN_LAG = MIX_LAG + 4
RING = 4
SCORE_BANKS = 3

PHASES = 2 * BATCH
AHEAD = 3
LOOP_FIRST, LOOP_PHASES = AHEAD, 2
TURNS = BATCH - AHEAD

FINISH_EARLY = (
    (1, "bias_input", 0), (3, "bias_input", 1), (9, "turn_attended", 0), (11, "turn_attended", 1),
    (14, "project_out", 0), (18, "project_out", 1), (19, "moments", 0), (20, "moments", 1), (21, "spread", 0),
    (23, "normalize", 0), (25, "bias_stream", 0), (26, "normalize", 1), (27, "bias_stream", 1),
    (28, "turn_normed", 0), (28, "turn_normed", 1), (29, "gates", 0), (31, "gates", 1), (34, "leaves", 0),
    (35, "leaves", 1), (36, "leaves", 2), (37, "leaves", 3), (39, "leaves", 4), (42, "turn_leaves", 0),
    (44, "turn_leaves", 1), (49, "mix", 0), (51, "mix", 1),
)
FINISH_LATE = (
    (1, "bias_input", 0), (1, "bias_input", 1), (22, "turn_attended", 0), (23, "turn_attended", 1),
    (30, "project_out", 0), (34, "project_out", 1), (35, "moments", 0), (37, "moments", 1), (39, "spread", 0),
    (44, "normalize", 0), (44, "normalize", 1), (45, "bias_stream", 0), (46, "turn_normed", 0),
    (46, "turn_normed", 1), (48, "bias_stream", 1), (49, "gates", 0), (49, "gates", 1), (51, "leaves", 0),
    (52, "leaves", 1), (53, "leaves", 2), (54, "leaves", 3), (55, "leaves", 4), (57, "turn_leaves", 0),
    (58, "turn_leaves", 1), (61, "mix", 0), (61, "mix", 1),
)
PREPARE_PLAIN = (
    (2, "moments", 0), (3, "moments", 1), (5, "spread", 0), (6, "normalize", 0), (8, "turn_normed", 0),
    (9, "normalize", 1), (11, "turn_normed", 1), (14, "heads_k", 0), (16, "heads_k", 1), (17, "high_k", 0),
    (17, "heads_q", 0), (17, "rest_k", 0), (18, "middle_k", 0), (18, "high_k", 1), (19, "heads_q", 1),
    (19, "high_q", 0), (19, "rest_k", 1), (20, "middle_k", 1), (21, "low_k", 0), (21, "low_k", 1), (22, "high_q", 1),
    (23, "rest_q", 0), (23, "rest_q", 1), (24, "middle_q", 0), (27, "low_q", 0), (28, "middle_q", 1),
    (32, "low_q", 1), (SLOTS + 2, "values", 0), (SLOTS + 4, "values", 1),
)
PREPARE_CAUSAL = (
    (0, "moments", 0), (2, "moments", 1), (3, "spread", 0), (5, "normalize", 0), (6, "normalize", 1),
    (7, "turn_normed", 0), (9, "turn_normed", 1), (11, "heads_k", 0), (11, "heads_k", 1), (12, "products_k", 0),
    (13, "products_k", 1), (14, "products_k", 2), (14, "products_k", 3), (15, "heads_q", 0), (16, "rotate_k", 0),
    (16, "rotate_k", 1), (16, "high_k", 0), (16, "products_q", 0), (16, "high_k", 1), (17, "heads_q", 1),
    (17, "rest_k", 0), (19, "products_q", 1), (19, "products_q", 2), (20, "middle_k", 0), (20, "products_q", 3),
    (20, "low_k", 0), (21, "rest_k", 1), (23, "middle_k", 1), (24, "rotate_q", 0), (24, "rotate_q", 1),
    (25, "low_k", 1), (25, "high_q", 0), (26, "high_q", 1), (26, "rest_q", 0), (27, "rest_q", 1), (27, "middle_q", 0),
    (28, "low_q", 0), (29, "middle_q", 1), (31, "low_q", 1), (SLOTS + 2, "values", 0), (SLOTS + 3, "values", 1),
)
PREPARE_FIRST = (
    ("moments", 0), ("spread", 0), ("normalize", 0), ("moments", 1), ("spread", 1), ("normalize", 1),
    ("turn_normed", 0), ("turn_normed", 1), ("heads_k", 0), ("heads_k", 1), ("high_k", 0), ("heads_q", 0),
    ("high_k", 1), ("heads_q", 1), ("rest_k", 0), ("rest_k", 1), ("middle_k", 0), ("high_q", 0), ("middle_k", 1),
    ("high_q", 1), ("low_k", 0), ("low_k", 1), ("rest_q", 0), ("rest_q", 1), ("middle_q", 0), ("middle_q", 1),
    ("low_q", 0), ("low_q", 1), ("values", 0), ("values", 1),
)
FINISH_LAST = (
    ("turn_attended", 0), ("turn_attended", 1), ("project_out", 0), ("moments", 0), ("spread", 0),
    ("project_out", 1), ("normalize", 0), ("moments", 1), ("spread", 1), ("normalize", 1), ("turn_normed", 0),
    ("bias_stream", 0), ("gates", 0), ("turn_normed", 1), ("bias_stream", 1), ("gates", 1),
    ("leaves", 0), ("leaves", 1), ("leaves", 2), ("leaves", 3), ("leaves", 4),
    ("leaves", 5), ("leaves", 6), ("leaves", 7), ("leaves", 8), ("leaves", 9),
    ("turn_leaves", 0), ("mix", 0), ("turn_leaves", 1), ("mix", 1),
)
LEAF_LEVELS = ((0, 1, 2, 3), (4, 5), (6,), (7,), (7,))

BANK_STEPS = ("turn_attended", "project_out", "turn_normed", "gates", "turn_leaves", "mix", "heads_k", "heads_q",
              "values")

PER_TURN = dict(
    scores_full=2 * 64, max_done=2 * 64, shift_full=2 * 4, shift_row=2 * 4, shift_sent0=2 * 2, shift_sent1=2 * 2,
    keyed_full=2 * 64, exp_done=2 * 64, causal_done=16, mixed_done=2 * 16, out_ready=2 * 4,
    out_turned=2 * 4, inverse_done=2 * 4, attended=2 * 4,
    moments_done=2 * 4, spread_done=2 * 2, variance=2 * 2, rstd=2 * 2, normed=2 * 4, turned_full=2 * 8,
    turned=2 * 8, added_full=2 * 4, x_ready=2 * 4, biased=2 * 3, gates_full=2 * 2, gates=2 * 2, level_done=2 * 9,
    heads_full=2 * 4, raw_ready=2 * 4, product_done=8, rotated=4, high=2 * 4, rest=2 * 4, middle=2 * 4, low=2 * 4,
    values_full=2 * 2, values_ready=2 * 2,
    stacked0=PLAIN_DMAS, stacked1=CAUSAL_DMAS, x_loaded=1, x_again=1, moved=1, kept=1, stored=1,
)


def causal(n):
    return n >= PHASES - AHEAD or (n >= AHEAD and n % 2 == AHEAD % 2)


def element(n):
    if n >= PHASES - AHEAD:
        return n - PHASES + BATCH
    return n if n < AHEAD else (n - AHEAD) // 2 + (0 if causal(n) else AHEAD)


def alone(n):
    return n < 0 or n >= PHASES


def tiles(i, n):
    return range(2 * i, 2 * i + 2) if alone(n) else range(TILES)


def schedule(n):
    due = {}
    if n > 0:
        for slot, step, i in FINISH_EARLY if causal(n) and not (n + 1 < PHASES and causal(n + 1)) else FINISH_LATE:
            due.setdefault(slot, []).append((step, i, n - 1))
    for m in (n, n + 1):
        if 0 < m < PHASES:
            for slot, step, i in PREPARE_CAUSAL if causal(m) else PREPARE_PLAIN:
                if slot // SLOTS == n + 1 - m:
                    due.setdefault(slot % SLOTS, []).append((step, i, m))
    return due


def score_unit(n, slot):
    n, unit = n + (slot + LEAD) // SLOTS, (slot + LEAD) % SLOTS
    return n, unit, unit // 16, unit % 16 // TILES, unit % TILES


def score_bank(n, unit):
    return (unit + n % 2) % SCORE_BANKS


def units_since(n, unit):
    before = [(p, u) for p in (n - 1, n) for u in range(SLOTS) if (p, u) < (n, unit)]
    return next(i for i, (p, u) in enumerate(reversed(before)) if score_bank(p, u) == score_bank(n, unit))


def shift_due(n, unit):
    return unit % 16 == SHIFT_LAG and 16 < n * SLOTS + unit < PHASES * SLOTS + 16


def out_due(n, slot):
    if slot % GROUP_SLOTS == (GROUP_SLOTS - GROUP + TURN_LAG) % GROUP_SLOTS and (n > 0 or slot >= TURN_LAG):
        return (slot // GROUP_SLOTS - (1 if TURN_LAG >= GROUP else 0)) % GROUPS
    return None


def work_banks():
    uses = [(step, i, 0, -1) for step, i in PREPARE_FIRST if step in BANK_STEPS]
    for n in range(PHASES + 1):
        for slot in range(-LEAD if n == 0 else 0, SLOTS if n < PHASES else 0):
            if shift_due(*score_unit(n, slot)[:2]):
                uses.append(("turn_max", n, slot))
            if slot >= 0:
                if out_due(n, slot) is not None:
                    uses.append(("turn_out", n, slot))
                uses += [(step, i, m, n) for step, i, m in schedule(n).get(slot, ()) if step in BANK_STEPS]
    uses.append(("turn_out", PHASES, 0))
    uses += [(step, i, PHASES - 1, PHASES) for step, i in FINISH_LAST if step in BANK_STEPS]
    return {use: at % 2 for at, use in enumerate(uses)}


class Count:

    def __init__(self):
        self.n = dict.fromkeys(PER_TURN, 0)
        self.turn = None
        self.last_read = {}

    def add(self, event, times=1):
        self.n[event] += times

    def some(self, event, back=0):
        return self.turn is not None or self.n[event] > back

    def of(self, event, back=0):
        n = self.n[event] - back
        return n if self.turn is None else self.turn * PER_TURN[event] + n

    def next(self, event):
        self.add(event)
        return self.of(event)

    def enter(self, turn):
        self.turn, self.start = turn, dict(self.n)

    def leave(self):
        self.turn = None
        for event, n in self.n.items():
            grown = n - self.start[event]
            assert grown in (0, PER_TURN[event]), (event, grown, PER_TURN[event])
            self.n[event] += grown * (TURNS - 1)
        for bank, (event, n) in self.last_read.items():
            self.last_read[bank] = event, n + PER_TURN[event] * (TURNS - 1)


def build(nc, x, w, out):
    with ExitStack() as ctx:
        def sb(name, shape, dt=F32):
            return ctx.enter_context(nc.sbuf_tensor(name, shape, dt))

        def bank(name, shape):
            return ctx.enter_context(nc.psum_tensor(name, shape, F32))

        def sem(name):
            return ctx.enter_context(nc.semaphore(name))

        weights = {k: sb(k, [P, KC, D]) for k in ("a_q", "a_k", "a_v", "a_o", "b_q", "b_k", "b_v", "b_o")}
        gate_w = sb("gate_w", [P, KC, D])
        leaf_w = sb("leaf_w", [P, KC, D])
        head_bias = {k: sb(k, [P, 2]) for k in ("a_q_bias", "a_k_bias")}
        wide_bias = {k: sb(k, [P, D]) for k in ("a_v_bias", "a_o_bias", "ffn_bias")}
        cosine = sb("cosine", [P, T])
        sine = sb("sine", [P, T])
        ident = sb("ident", [P, P])
        ident_b = sb("ident_b", [P, P], BF16)
        mask_b = sb("mask_b", [P, P], BF16)
        minus_half = sb("minus_half", [P, TILES])

        x_in = sb("x_in", [P, TILES, D])
        x_again = sb("x_again", [P, TILES, D])
        x_plain = sb("x_plain", [P, TILES, D])
        x_moved = sb("x_moved", [P, TILES, D])
        x_kept = sb("x_kept", [P, TILES, D])
        x_causal = sb("x_causal", [P, TILES, D])

        q_stack = [sb(f"q_stack{s}", [P, HEADS, T], BF16) for s in range(2)]
        k_stack = [sb(f"k_stack{s}", [P, HEADS, T], BF16) for s in range(2)]
        v_flat = [sb(f"v_ones{s}", [P, TILES * HEADS * VALUE + COLS - VALUE]) for s in range(2)]

        def values_of(s):
            return v_flat[s][:, 0:TILES * HEADS * VALUE].rearrange("p (t h d) -> p t h d", t=TILES, h=HEADS)

        turned_heads = sb("turned_heads", [P, KC, T])
        turned_block = sb("turned_block", [P, KC, T])
        attended = sb("attended", [P, TILES, D])
        parts = {k: [sb(f"{k}_part{i}", [P, 2, T], BF16) for i in range(3)] for k in "qk"}
        scratch = sb("scratch", [P, 5, 1024])
        probs = [sb(f"probs{i}", [P, GROUP, T]) for i in range(RING)]
        out_raw = [sb(f"out_raw{i}", [P, T]) for i in range(2)]
        neg_max = [sb(f"neg_max{i}", [P, TILES, GROUP], BF16) for i in range(2)]
        shift_rows = [sb(f"shift_rows{i}", [GROUP, T], BF16) for i in range(2)]
        inverse = sb("inverse", [P, TILES, GROUP])
        moments = sb("moments", [P, TILES, 6])
        spread = sb("spread", [P, TILES, 2])
        variance = sb("variance", [P, TILES])
        rstd = sb("rstd", [P, TILES])

        def tiles_of(i):
            return scratch[:, i, :].rearrange("p (t n) -> p t n", t=TILES)

        def halves_of(i):
            return scratch[:, i, :].rearrange("p (c n) -> p c n", c=2)

        def staged(i, n):
            room = (x_kept, x_causal)[i // 2][:, 2 * (i % 2):2 * (i % 2) + 2, :].rearrange("p t n -> p (t n)")
            return room[:, 0:KC * n].rearrange("p (k n) -> p k n", k=KC)

        normed_block, tanh_gates, leaf_probs = tiles_of(0), tiles_of(0), [tiles_of(1), tiles_of(2)]
        raw = dict(k=halves_of(0), q=halves_of(3))
        by_cos, by_sin = halves_of(1), halves_of(2)
        normed_heads = tiles_of(4)

        def rest_of(which, m):
            return halves_of(1) if which == "q" and not causal(m) else halves_of(4)

        ps_max = [bank(f"ps_max{i}", [P, T]) for i in range(SCORE_BANKS)]
        ps_key = [bank(f"ps_key{i}", [P, T]) for i in range(2)]
        ps_out = bank("ps_out", [P, T])
        ps_work = [bank(f"ps_work{i}", [P, T]) for i in range(2)]
        bank_of = {use: ps_work[i] for use, i in work_banks().items()}

        def by_tile(bank):
            return bank[:, :].rearrange("p (t n) -> p t n", t=2)

        def by_head(bank):
            return bank[:, :].rearrange("p (q j c) -> p q j c", q=TILES, j=GROUP)

        def as_rows(bank):
            return bank[0:GROUP, 0:T // 2].bitcast(BF16)

        on = {name: sem(name) for name in PER_TURN}
        first_loaded = sem("first_loaded")
        fold_loaded = sem("fold_loaded")
        rest_loaded = sem("rest_loaded")
        zeroed = sem("zeroed")
        constants = sem("constants")
        rounded = sem("rounded")
        ones_made = sem("ones_made")
        ones_set = sem("ones_set")
        fold_full = sem("fold_full")
        folded = sem("folded")
        FIRST = ("a_k", "a_q", "a_v", "a_k_bias", "a_q_bias", "a_v_bias")
        FOLD = ("ffn_q", "routers", "leaf_values", "ffn_o")
        REST = ("a_o", "b_q", "b_k", "b_v", "b_o", "a_o_bias", "ffn_bias", "cosine", "sine")
        block = ctx.enter_context(nc.Block())

        def load_weight(eng, name, loaded):
            by_rows = lambda ap: ap.rearrange("(k p) n -> p k n", p=P)
            if name in weights:
                dst, src = weights[name][:, :, :], by_rows(w[name])
            elif name in head_bias:
                dst, src = head_bias[name][:, :], w[name]
            elif name in wide_bias:
                dst, src = wide_bias[name][:, :], w[name].partition_broadcast(P)
            elif name in ("cosine", "sine"):
                dst, src = (cosine if name == "cosine" else sine)[:, :], w[name]
            else:
                at = FOLD.index(name)
                dst, src = staged(at, w[name].shape[1]), by_rows(w[name])
            eng.dma_start(dst, src).then_inc(loaded, DMA)

        def program(eng, count, core, steps, opening, closing):
            def phase(n):
                due = schedule(n)
                for slot in range(SLOTS):
                    core(n, slot)
                    for step, i, m in due.get(slot, ()):
                        if step in steps:
                            steps[step](m, i, n, bank_of.get((step, i, m, n)))

            for step, i in PREPARE_FIRST:
                if step in steps:
                    steps[step](0, i, -1, bank_of.get((step, i, 0, -1)))
            opening()
            for n in range(LOOP_FIRST):
                phase(n)
            with eng.Fori(0, TURNS) as turn:
                count.enter(turn)
                for n in range(LOOP_FIRST, LOOP_FIRST + LOOP_PHASES):
                    phase(n)
            count.leave()
            for n in range(LOOP_FIRST + TURNS * LOOP_PHASES, PHASES):
                phase(n)
            closing()
            for step, i in FINISH_LAST:
                if step in steps:
                    steps[step](PHASES - 1, i, PHASES, bank_of.get((step, i, PHASES - 1, PHASES)))

        def stream(m, n):
            if n >= m:
                return x_causal if causal(m) else x_plain
            return x_in if not causal(m) else x_moved if m < PHASES - 1 else x_plain

        def kept(m):
            return x_kept if m < PHASES - 2 else x_moved if m < PHASES - 1 else x_plain

        @block.sync
        def _(sp):
            count = Count()

            def one(tensor, e):
                got = tensor[e] if count.turn is None else tensor[bass.ds(count.turn + e, 1)].squeeze(0)
                return got.rearrange("(t p) d -> p t d", p=P)

            def load_x(m):
                if count.some("normed"):
                    sp.wait_ge(on["normed"], count.of("normed"))
                    sp.nop(nofuse=True)
                sp.dma_start(x_in[:, :, :], one(x, element(m))).then_inc(on["x_loaded"], DMA)

            def load_again(m):
                if count.some("x_ready"):
                    sp.wait_ge(on["x_ready"], count.of("x_ready"))
                    sp.nop(nofuse=True)
                sp.dma_start(x_again[:, :, :], one(x, element(m))).then_inc(on["x_again"], DMA)

            def core(n, slot):
                if slot == 0:
                    if n > 0:
                        count.add("keyed_full", SLOTS)
                    if n + 1 < PHASES and not causal(n + 1):
                        load_x(n + 1)
                if slot == 40 and not causal(n):
                    load_again(n)

            def stack(m, which, part):
                dst = (q_stack if which == "q" else k_stack)[m % 2]
                held = on["stacked0"] if m % 2 == 0 else on["stacked1"]
                for r, holds in enumerate(QUERY_PARTS if which == "q" else KEY_PARTS):
                    if holds == part and causal(m):
                        for c in range(2):
                            row = DH * r + PAIRS * c
                            sp.dma_start(dst[row:row + PAIRS, :, :], parts[which][part][:, c, :]).then_inc(held, DMA)
                    elif holds == part:
                        sp.dma_start(dst[DH * r:DH * r + DH, :, :], parts[which][part][:, :, :]).then_inc(held, DMA)

            def stack_high(which):
                def step(m, i, n, bank):
                    count.add("high")
                    if i == 0:
                        return
                    if count.some("keyed_full"):
                        sp.wait_ge(on["keyed_full"], count.of("keyed_full"))
                        sp.nop(nofuse=True)
                    sp.wait_ge(on["high"], count.of("high"))
                    sp.nop(nofuse=True)
                    stack(m, which, 0)
                return step

            def stack_middle(which):
                def step(m, i, n, bank):
                    count.add("middle")
                    if i == 1:
                        sp.wait_ge(on["middle"], count.of("middle"))
                        sp.nop(nofuse=True)
                        stack(m, which, 1)
                return step

            def stack_low(which):
                def step(m, i, n, bank):
                    count.add("low")
                    if i == 1:
                        sp.wait_ge(on["low"], count.of("low"))
                        sp.nop(nofuse=True)
                        stack(m, which, 2)
                return step

            def normalize(m, i, n, bank):
                count.add("normed")

            def move():
                sp.wait_ge(on["x_ready"], count.of("x_ready"))
                sp.nop(nofuse=True)
                sp.wait_ge(on["normed"], count.of("normed"))
                sp.nop(nofuse=True)
                if count.some("kept"):
                    sp.wait_ge(on["kept"], count.of("kept") * DMA)
                    sp.nop(nofuse=True)
                sp.dma_start(x_moved[:, :, :], x_plain[:, :, :]).then_inc(on["moved"], DMA)
                count.add("moved")

            def keep():
                sp.wait_ge(on["x_ready"], count.of("x_ready"))
                sp.nop(nofuse=True)
                sp.wait_ge(on["moved"], count.of("moved") * DMA)
                sp.nop(nofuse=True)
                sp.dma_start(x_kept[:, :, :], x_moved[:, :, :]).then_inc(on["kept"], DMA)
                count.add("kept")

            def project_out(m, i, n, bank):
                count.add("x_ready")
                if i == 1 and causal(m) and n < PHASES - AHEAD:
                    keep()
                    move()

            def mix(m, i, n, bank):
                count.add("x_ready")
                if i == 1 and m == 1:
                    keep()
                if i == 1 and m < 2:
                    move()
                if causal(m) and (i == 1 or alone(n)):
                    sp.wait_ge(on["x_ready"], count.of("x_ready"))
                    sp.nop(nofuse=True)
                    some = tiles(i, n)
                    sp.dma_start(one(out, element(m))[:, some[0]:some[-1] + 1, :],
                                 x_causal[:, some[0]:some[-1] + 1, :]).then_inc(on["stored"], DMA)
                    count.add("stored")

            def opening():
                pass

            sp.sem_inc(on["stored"], DMA)
            count.add("stored")
            load_x(0)
            for name in FIRST:
                load_weight(sp, name, first_loaded)
            for name in FOLD:
                load_weight(sp, name, fold_loaded)
            for name in REST:
                load_weight(sp, name, rest_loaded)
            program(sp, count, core, dict(high_k=stack_high("k"), middle_k=stack_middle("k"),
                                          low_k=stack_low("k"), high_q=stack_high("q"),
                                          middle_q=stack_middle("q"), low_q=stack_low("q"),
                                          normalize=normalize, project_out=project_out, mix=mix),
                    opening, opening)
            sp.wait_ge(on["stored"], count.of("stored") * DMA)

        @block.gpsimd
        def _(pool):
            count = Count()
            for t in (ident, mask_b):
                pool.memset(t[:, :], 0.0).then_inc(zeroed, 1)
            pool.memset(minus_half[:, :], -0.5).then_inc(zeroed, 1)
            for s in range(2):
                pool.memset(v_flat[s][:, TILES * HEADS * VALUE:], 0.0).then_inc(zeroed, 1)
                pool.memset(values_of(s)[:, :, :, DH:VALUE], 1.0).then_inc(constants, 1)
            pool.wait_ge(zeroed, 5)
            pool.affine_select(out=ident[:, :], in_=ident[:, :], compare_op=ALU.not_equal, fill=1.0, base=0,
                               pattern=[[-1, P]], channel_multiplier=1).then_inc(constants, 1)
            pool.affine_select(out=mask_b[:, :], in_=mask_b[:, :], compare_op=ALU.is_ge, fill=MASKED, base=0,
                               pattern=[[-1, P]], channel_multiplier=1).then_inc(constants, 1)
            ones = parts["k"][2][0:HEADS, 0, :]
            pool.memset(ones, 1.0).then_inc(ones_made, 1)
            pool.wait_ge(ones_made, 1)
            for s in range(2):
                pool.dma_start(k_stack[s][SHIFT_ROW:STACK_ROWS, :, :], ones).then_inc(ones_set, DMA)

            def send_shift(n, slot):
                n, unit, g, _, _ = score_unit(n, slot)
                if not shift_due(n, unit):
                    return
                n, g = (n, g - 1) if g else (n - 1, GROUPS - 1)
                pool.wait_ge(on["shift_row"], count.next("shift_row"))
                pool.nop(nofuse=True)
                sent = on["shift_sent0"] if g % 2 == 0 else on["shift_sent1"]
                pool.dma_start(q_stack[n % 2][SHIFT_ROW:STACK_ROWS, GROUP * g:GROUP * (g + 1), :],
                               shift_rows[g % 2][:, :]).then_inc(sent, DMA)

            def core(n, slot):
                send_shift(n, slot)
                step, r = slot // 4, slot % 4
                if r == 3:
                    count.add("exp_done", GROUP)
                    if causal(n):
                        kb = step % TILES
                        tile = probs[step % RING][:, :, P * kb:P * kb + P]
                        pool.wait_ge(on["exp_done"], count.of("exp_done"))
                        pool.nop(nofuse=True)
                        pool.affine_select(out=tile, in_=tile, compare_op=ALU.is_ge, fill=0.0, base=0,
                                           pattern=[[0, GROUP], [1, P]], channel_multiplier=-1)\
                            .then_inc(on["causal_done"], 1)

            def add_bias(dst, i, bias):
                two = dst[:, 2 * i:2 * i + 2, :]
                row = wide_bias[bias][:, :].unsqueeze(1).broadcast_to([P, 2, D])
                pool.tensor_tensor(two, two, row, ALU.add).then_inc(on["biased"], 1)

            def bias_input(m, i, n, bank):
                if not causal(m):
                    if i == 0:
                        pool.wait_ge(on["x_again"], count.next("x_again") * DMA)
                        pool.nop(nofuse=True)
                    add_bias(x_again, i, "a_o_bias")

            def spread_step(m, i, n, bank):
                pool.wait_ge(on["variance"], count.next("variance"))
                pool.nop(nofuse=True)
                some = slice(tiles(i, n)[0], tiles(i, n)[-1] + 1)
                pool.tensor_tensor(rstd[:, some], variance[:, some], minus_half[:, some], ALU.pow)\
                    .then_inc(on["rstd"], 1)

            def normalize(m, i, n, bank):
                count.add("normed")

            def bias_stream(m, i, n, bank):
                pool.wait_ge(on["normed"], count.of("normed"))
                pool.nop(nofuse=True)
                add_bias(stream(m, n), i, "ffn_bias")

            def products(which):
                def step(m, i, n, bank):
                    if not causal(m):
                        return
                    c = i // 2
                    if i % 2 == 0:
                        pool.wait_ge(on["raw_ready"], count.next("raw_ready"))
                        pool.nop(nofuse=True)
                    if i == 0 and count.some("rotated"):
                        pool.wait_ge(on["rotated"], count.of("rotated"))
                        pool.nop(nofuse=True)
                    dst, factor = (by_sin, sine) if i % 2 else (by_cos, cosine)
                    pool.tensor_tensor(dst[:, c, :], raw[which][:, c, :], factor[:, :], ALU.mult)\
                        .then_inc(on["product_done"], 1)
                return step

            def heads(m, i, n, bank):
                if not causal(m):
                    count.add("raw_ready")

            def rotate(m, i, n, bank):
                if causal(m):
                    count.add("rotated")

            def low_part(which):
                def step(m, i, n, bank):
                    if m == 0 and which == "k" and i == 0:
                        pool.wait_ge(ones_set, 2 * DMA)
                    pool.wait_ge(on["middle"], count.next("middle"))
                    pool.nop(nofuse=True)
                    pool.tensor_tensor(parts[which][2][:, i, :], rest_of(which, m)[:, i, :], parts[which][1][:, i, :],
                                       ALU.subtract).then_inc(on["low"], 1)
                return step

            def opening():
                pool.wait_ge(rest_loaded, DMA * len(REST))
                for slot in range(-LEAD, 0):
                    send_shift(0, slot)

            def closing():
                pass

            program(pool, count, core, dict(bias_input=bias_input, spread=spread_step, normalize=normalize,
                                            bias_stream=bias_stream, heads_k=heads, heads_q=heads,
                                            products_k=products("k"), products_q=products("q"),
                                            rotate_k=rotate, rotate_q=rotate, low_k=low_part("k"),
                                            low_q=low_part("q")), opening, closing)

        @block.scalar
        def _(act):
            count = Count()
            act.wait_ge(constants, 4)
            act.activation(ident_b[:, :], ident[:, :], ACT.Copy).then_inc(rounded, 1)
            act.wait_ge(first_loaded, DMA * len(FIRST))

            def core(n, slot):
                step, j = slot // GROUP, slot % GROUP
                kb = step % TILES
                q0 = P * kb if causal(n) else 0
                if j == 0:
                    if count.some("mixed_done", RING - 1):
                        act.wait_ge(on["mixed_done"], count.of("mixed_done", RING - 1))
                    count.add("mixed_done")
                act.wait_ge(on["keyed_full"], count.next("keyed_full"))
                act.activation(probs[step % RING][:, j, q0:T], ps_key[slot % 2][:, 0:T - q0], ACT.Exp,
                               scale=SCALE).then_inc(on["exp_done"], 1)
                ended = (GROUP_SLOTS - GROUP + OUT_LAG) % GROUP_SLOTS
                if slot % GROUP_SLOTS == ended and (n > 0 or slot >= GROUP_SLOTS):
                    copy_out((slot // GROUP_SLOTS - 1) % GROUPS, OUT_LAG // GROUP)

            def copy_out(g, begun):
                act.wait_ge(on["mixed_done"], count.of("mixed_done", begun))
                act.activation(out_raw[g % 2][:, :], ps_out[:, :], ACT.Copy).then_inc(on["out_ready"], 1)

            def opening():
                pass

            def closing():
                copy_out(GROUPS - 1, 0)

            def turn(m, i, n, bank):
                act.wait_ge(on["turned_full"], count.next("turned_full"))
                dst = turned_heads if n < m else turned_block
                act.activation(dst[:, :, 2 * P * i:2 * P * i + 2 * P],
                               bank[:, :].rearrange("p (k n) -> p k n", k=KC), ACT.Copy).then_inc(on["turned"], 1)

            def gates(m, i, n, bank):
                act.wait_ge(on["gates_full"], count.next("gates_full"))
                act.activation(tanh_gates[:, 2 * i:2 * i + 2, 0:NODES], by_tile(bank)[:, :, 0:NODES], ACT.Tanh,
                               scale=0.5).then_inc(on["gates"], 1)

            def heads(which):
                def step(m, i, n, bank):
                    act.wait_ge(on["heads_full"], count.next("heads_full"))
                    dst = raw[which][:, i, :]
                    if causal(m):
                        act.activation(dst, bank[:, :], ACT.Copy).then_inc(on["raw_ready"], 1)
                    else:
                        act.activation(dst, bank[:, :], ACT.Identity,
                                       bias=head_bias[f"a_{which}_bias"][:, i:i + 1]).then_inc(on["raw_ready"], 1)
                    count.add("raw_ready")
                return step

            def high_part(which):
                def step(m, i, n, bank):
                    if causal(m):
                        act.wait_ge(on["rotated"], count.next("rotated"))
                    else:
                        act.wait_ge(on["raw_ready"], count.of("raw_ready"))
                    act.activation(parts[which][0][:, i, :], raw[which][:, i, :], ACT.Copy).then_inc(on["high"], 1)
                return step

            def middle_part(which):
                def step(m, i, n, bank):
                    act.wait_ge(on["rest"], count.next("rest"))
                    act.activation(parts[which][1][:, i, :], rest_of(which, m)[:, i, :], ACT.Copy)\
                       .then_inc(on["middle"], 1)
                return step

            def values(m, i, n, bank):
                count.add("values_full")
                if causal(m):
                    act.wait_ge(on["values_full"], count.of("values_full"))
                    act.activation(values_of(m % 2)[:, 2 * i:2 * i + 2, :, 0:DH],
                                   by_tile(bank).rearrange("p t (h d) -> p t h d", h=HEADS), ACT.Copy)\
                       .then_inc(on["values_ready"], 1)

            program(act, count, core, dict(turn_attended=turn, turn_normed=turn, turn_leaves=turn, gates=gates,
                                           heads_k=heads("k"), heads_q=heads("q"), high_k=high_part("k"),
                                           high_q=high_part("q"), middle_k=middle_part("k"),
                                           middle_q=middle_part("q"), values=values), opening, closing)

        @block.vector
        def _(dve):
            count = Count()
            def largest(n, slot):
                at = n, slot
                n, unit, g, j, qt = score_unit(n, slot)
                if n < PHASES:
                    keys = P * (qt + 1) if causal(n) else T
                    dve.wait_ge(on["scores_full"], count.next("scores_full"))
                    dve.tensor_reduce(out=neg_max[g % 2][:, qt, j:j + 1], in_=ps_max[score_bank(n, unit)][:, 0:keys],
                                      axis=AX_X, op=ALU.max, negate=True).then_inc(on["max_done"], 1)
                if shift_due(n, unit):
                    h, bank = (g + 1) % 2, bank_of["turn_max", *at]
                    sent = on["shift_sent0"] if h == 0 else on["shift_sent1"]
                    dve.wait_ge(on["shift_full"], count.next("shift_full"))
                    if count.some(f"shift_sent{h}"):
                        dve.wait_ge(sent, count.of(f"shift_sent{h}") * DMA)
                    count.add(f"shift_sent{h}")
                    dve.tensor_copy(shift_rows[h][:, :], as_rows(bank)).then_inc(on["shift_row"], 1)

            def divide(g, bank):
                turned = by_head(bank)
                if count.some("attended"):
                    dve.wait_ge(on["attended"], count.of("attended"))
                count.add("attended")
                dve.wait_ge(on["out_turned"], count.next("out_turned"))
                dve.reciprocal(inverse[:, :, :], turned[:, :, :, DH]).then_inc(on["inverse_done"], 1)
                dve.wait_ge(on["inverse_done"], count.next("inverse_done"))
                dst = attended[:, :, GROUP * DH * g:GROUP * DH * (g + 1)].rearrange("p q (j d) -> p q j d", j=GROUP)
                dve.tensor_tensor(dst, turned[:, :, :, 0:DH],
                                  inverse[:, :, :].unsqueeze(3).broadcast_to([P, TILES, GROUP, DH]), ALU.mult)\
                   .then_inc(on["attended"], 1)

            def core(n, slot):
                largest(n, slot)
                if out_due(n, slot) is not None:
                    divide(out_due(n, slot), bank_of["turn_out", n, slot])

            def opening():
                dve.wait_ge(fold_full, 1)
                for c in range(KC):
                    dve.tensor_copy(gate_w[:, c, 0:NODES], ps_max[c][:, 0:NODES]).then_inc(folded, 1)
                    dve.tensor_scalar(leaf_w[:, c, :], ps_key[c][:, 0:D], 2.0 ** -LEVELS, None, ALU.mult)\
                       .then_inc(folded, 1)
                for slot in range(-LEAD, 0):
                    largest(0, slot)

            def closing():
                divide(GROUPS - 1, bank_of["turn_out", PHASES, 0])

            def add(m, i, bank, src):
                two = slice(2 * i, 2 * i + 2)
                dst = x_causal if causal(m) else x_plain
                dve.wait_ge(on["added_full"], count.next("added_full"))
                dve.tensor_tensor(dst[:, two, :], by_tile(bank), src[:, two, :], ALU.add).then_inc(on["x_ready"], 1)
                count.add("x_ready")

            def project_out(m, i, n, bank):
                if i == 0 and causal(m):
                    dve.wait_ge(on["kept"], count.of("kept") * DMA)
                    dve.wait_ge(on["stored"], count.next("stored") * DMA)
                elif not causal(m):
                    dve.wait_ge(on["biased"], count.next("biased"))
                    if i == 0 and count.some("moved"):
                        dve.wait_ge(on["moved"], count.of("moved") * DMA)
                add(m, i, bank, kept(m) if causal(m) else x_again)
                if i == 1 and causal(m) and n < PHASES - AHEAD:
                    count.add("kept")
                    count.add("moved")

            def mix(m, i, n, bank):
                dve.wait_ge(on["biased"], count.next("biased"))
                add(m, i, bank, stream(m, n))
                if i == 1 and m < 2:
                    count.add("moved")
                    count.add("kept", m)

            def moments_step(m, i, n, bank):
                src = stream(m, n)
                if src is x_in and i == 0:
                    dve.wait_ge(on["x_loaded"], count.next("x_loaded") * DMA)
                elif src is x_moved and i == 0:
                    dve.wait_ge(on["moved"], count.of("moved") * DMA)
                elif n >= m or m == PHASES - 1:
                    dve.wait_ge(on["x_ready"], count.of("x_ready"))
                for t in (2 * i, 2 * i + 1):
                    last = dve.bn_stats(moments[:, t, :], src[:, t, :])
                last.then_inc(on["moments_done"], 1)
                count.add("moments_done")

            def spread_step(m, i, n, bank):
                dve.wait_ge(on["moments_done"], count.of("moments_done"))
                dve.nop(nofuse=True)
                some = tiles(i, n)
                for t in some:
                    last = dve.bn_aggr(spread[:, t, :], moments[:, t, :])
                last.then_inc(on["spread_done"], 1)
                dve.wait_ge(on["spread_done"], count.next("spread_done"))
                some = slice(some[0], some[-1] + 1)
                dve.tensor_scalar(variance[:, some], spread[:, some, 1], EPS, None, ALU.add)\
                   .then_inc(on["variance"], 1)

            def normalize(m, i, n, bank):
                src = stream(m, n)
                if i == 0 or alone(n):
                    dve.wait_ge(on["rstd"], count.next("rstd"))
                if i == 0:
                    if n < m and count.some("low"):
                        dve.wait_ge(on["low"], count.of("low"))
                    elif n >= m and count.some("rest"):
                        dve.wait_ge(on["rest"], count.of("rest"))
                dst = normed_heads if n < m else normed_block
                for t in (2 * i, 2 * i + 1):
                    last = dve.tensor_scalar(dst[:, t, :], src[:, t, :], spread[:, t, 0:1], rstd[:, t:t + 1],
                                             ALU.subtract, ALU.mult)
                last.then_inc(on["normed"], 1)

            def leaves(m, i, n, bank):
                some, i = tiles(i // len(LEAF_LEVELS), n), i % len(LEAF_LEVELS)
                if i == 0:
                    count.add("gates", len(some) // 2)
                    dve.wait_ge(on["gates"], count.of("gates"))
                    dve.wait_ge(on["low"], count.of("low"))
                some = slice(some[0], some[-1] + 1)
                for level in LEAF_LEVELS[i]:
                    nodes = 2 ** level
                    gate = tanh_gates[:, some, nodes - 1:2 * nodes - 1]
                    above = leaf_probs[(level + 1) % 2][:, some, 0:nodes]
                    below = leaf_probs[level % 2][:, some, 0:2 * nodes].rearrange("p t (n s) -> p t n s", s=2)
                    left, right = level < LEVELS - 1 or i == 3, level < LEVELS - 1 or i == 4
                    if level == 0:
                        dve.tensor_scalar(below[:, :, :, 0], gate, -1.0, 1.0, ALU.mult, ALU.add)
                        last = dve.tensor_scalar(below[:, :, :, 1], gate, 1.0, None, ALU.add)
                    else:
                        dve.wait_ge(on["level_done"], count.of("level_done"))
                        if left:
                            last = dve.scalar_tensor_tensor(out=below[:, :, :, 0], in0=gate, scalar=1.0, in1=above,
                                                            op0=ALU.subtract, op1=ALU.mult, reverse0=True)
                        if right:
                            last = dve.scalar_tensor_tensor(out=below[:, :, :, 1], in0=gate, scalar=1.0, in1=above,
                                                            op0=ALU.add, op1=ALU.mult)
                    last.then_inc(on["level_done"], 1)
                    count.add("level_done")

            def rotate(which):
                def step(m, i, n, bank):
                    if not causal(m):
                        return
                    if i == 0:
                        count.add("product_done", 4)
                        dve.wait_ge(on["product_done"], count.of("product_done"))
                        dve.tensor_tensor(raw[which][:, 0, :], by_cos[:, 0, :], by_sin[:, 1, :], ALU.subtract)\
                           .then_inc(on["rotated"], 1)
                    else:
                        dve.tensor_tensor(raw[which][:, 1, :], by_sin[:, 0, :], by_cos[:, 1, :], ALU.add)\
                           .then_inc(on["rotated"], 1)
                return step

            def rest_part(which):
                def step(m, i, n, bank):
                    dve.wait_ge(on["high"], count.next("high"))
                    if which == "q" and causal(m):
                        dve.wait_ge(on["low"], count.of("low"))
                    dve.tensor_tensor(rest_of(which, m)[:, i, :], raw[which][:, i, :], parts[which][0][:, i, :],
                                      ALU.subtract).then_inc(on["rest"], 1)
                    count.add("rest")
                return step

            def low_step(m, i, n, bank):
                count.add("low")

            def values(m, i, n, bank):
                dst = values_of(m % 2)[:, 2 * i:2 * i + 2, :, 0:DH]
                src = by_tile(bank).rearrange("p t (h d) -> p t h d", h=HEADS)
                if m == 0 and i == 0:
                    dve.wait_ge(first_loaded, DMA * len(FIRST))
                count.add("values_full")
                if not causal(m):
                    dve.wait_ge(on["values_full"], count.of("values_full"))
                    bias = wide_bias["a_v_bias"][:, :].rearrange("p (h d) -> p h d", h=HEADS).unsqueeze(1)
                    dve.tensor_tensor(dst, src, bias.broadcast_to([P, 2, HEADS, DH]), ALU.add)\
                       .then_inc(on["values_ready"], 1)

            program(dve, count, core, dict(project_out=project_out, mix=mix, moments=moments_step, spread=spread_step,
                                           normalize=normalize, leaves=leaves, rotate_k=rotate("k"),
                                           rotate_q=rotate("q"), rest_k=rest_part("k"), rest_q=rest_part("q"),
                                           low_k=low_step, low_q=low_step, values=values),
                    opening, closing)

        @block.tensor
        def _(pe):
            count = Count()
            def take(bank, event):
                if bank.name in count.last_read:
                    read, n = count.last_read[bank.name]
                    pe.wait_ge(on[read], count.of(read, count.n[read] - n))
                count.add(event)
                count.last_read[bank.name] = event, count.n[event]

            pe.wait_ge(constants, 4)
            pe.wait_ge(rounded, 1)
            pe.wait_ge(first_loaded, DMA * len(FIRST))

            def scores(n, unit, g, j, qt):
                if unit == 0:
                    held = on["stacked0"] if n % 2 == 0 else on["stacked1"]
                    count.add(f"stacked{n % 2}", CAUSAL_DMAS if causal(n) else PLAIN_DMAS)
                    pe.wait_ge(held, count.of(f"stacked{n % 2}") * DMA)
                h = GROUP * g + j
                keys = P * (qt + 1) if causal(n) else T
                back = units_since(n, unit)
                if count.some("max_done", back):
                    pe.wait_ge(on["max_done"], count.of("max_done", back))
                count.add("max_done")
                dst = ps_max[score_bank(n, unit)]
                last = pe.matmul(dst[:, 0:keys], q_stack[n % 2][0:SPLIT_ROWS, h, P * qt:P * qt + P],
                                 k_stack[n % 2][0:SPLIT_ROWS, h, 0:keys], start=True, stop=not causal(n))
                if causal(n):
                    last = pe.matmul(dst[:, keys - P:keys], ident_b[:, :], mask_b[:, :], start=False, stop=True)
                last.then_inc(on["scores_full"], 1)

            def turn_max(g, begun, bank):
                pe.wait_ge(on["max_done"], count.of("max_done", begun))
                take(bank, "shift_row")
                for qt in range(TILES):
                    last = pe.transpose(as_rows(bank)[:, P * qt:P * qt + P], neg_max[g % 2][:, qt, :], ident_b[:, :])
                last.then_inc(on["shift_full"], 1)

            def ahead(n, slot):
                at = n, slot
                n, unit, g, j, qt = score_unit(n, slot)
                if n < PHASES:
                    scores(n, unit, g, j, qt)
                if shift_due(n, unit):
                    turn_max((g - 1) % GROUPS, SHIFT_LAG + 1 if n < PHASES else 0, bank_of["turn_max", *at])

            def by_key(n, slot):
                step, j = slot // GROUP, slot % GROUP
                g, kb = step // TILES, step % TILES
                q0 = P * kb if causal(n) else 0
                if kb == 0 and j == 0:
                    sent = on["shift_sent0"] if g % 2 == 0 else on["shift_sent1"]
                    pe.wait_ge(sent, count.next(f"shift_sent{g % 2}") * DMA)
                if count.some("exp_done", 1):
                    pe.wait_ge(on["exp_done"], count.of("exp_done", 1))
                count.add("exp_done")
                h = GROUP * g + j
                pe.matmul(ps_key[slot % 2][:, 0:T - q0], k_stack[n % 2][0:STACK_ROWS, h, P * kb:P * kb + P],
                          q_stack[n % 2][0:STACK_ROWS, h, q0:T], start=True, stop=True).then_inc(on["keyed_full"], 1)

            def mixed(n, step, begun):
                g, kb = step // TILES, step % TILES
                q0 = P * kb if causal(n) else 0
                if causal(n):
                    pe.wait_ge(on["causal_done"], count.next("causal_done"))
                else:
                    pe.wait_ge(on["exp_done"], count.of("exp_done", begun))
                if step == 0:
                    pe.wait_ge(on["values_ready"], count.of("values_ready"))
                if kb == 0:
                    if count.some("out_ready"):
                        pe.wait_ge(on["out_ready"], count.of("out_ready"))
                    count.add("out_ready")
                for j in range(GROUP):
                    at = VALUE * (HEADS * kb + GROUP * g + j)
                    last = pe.matmul(ps_out[COLS * j:COLS * j + COLS, q0:T], v_flat[n % 2][:, at:at + COLS],
                                     probs[step % RING][:, j, q0:T], start=(kb == 0), stop=(kb == TILES - 1),
                                     tile_position=(0, COLS * j))
                last.then_inc(on["mixed_done"], 1)

            def turn_out(g, bank):
                pe.wait_ge(on["out_ready"], count.of("out_ready"))
                take(bank, "attended")
                for qt in range(TILES):
                    last = pe.transpose(bank[:, P * qt:P * qt + P], out_raw[g % 2][:, P * qt:P * qt + P], ident[:, :])
                last.then_inc(on["out_turned"], 1)

            def core(n, slot):
                ahead(n, slot)
                if out_due(n, slot) is not None:
                    turn_out(out_due(n, slot), bank_of["turn_out", n, slot])
                by_key(n, slot)
                if slot % GROUP == MIX_LAG % GROUP:
                    step = (slot - MIX_LAG) // GROUP
                    if step >= 0:
                        mixed(n, step, MIX_LAG - GROUP + 1)
                    elif n > 0:
                        mixed(n - 1, step + STEPS, MIX_LAG - GROUP + 1)

            def opening():
                pe.wait_ge(fold_loaded, DMA * len(FOLD))
                for c in range(KC):
                    for k in range(KC):
                        pe.matmul(ps_max[c][:, 0:NODES], staged(0, D)[:, k, P * c:P * c + P], staged(1, NODES)[:, k, :],
                                  start=(k == 0), stop=(k == KC - 1))
                for c in range(KC):
                    for k in range(KC):
                        last = pe.matmul(ps_key[c][:, 0:D], staged(2, D)[:, k, P * c:P * c + P], staged(3, D)[:, k, :],
                                         start=(k == 0), stop=(k == KC - 1))
                last.then_inc(fold_full, 1)
                pe.wait_ge(folded, 4)
                pe.wait_ge(ones_set, 2 * DMA)
                for slot in range(-LEAD, 0):
                    ahead(0, slot)

            def closing():
                for late in range(MIX_LAG // GROUP):
                    step = STEPS - MIX_LAG // GROUP + late
                    mixed(PHASES - 1, step, SLOTS - GROUP * (step + 1))
                turn_out(GROUPS - 1, bank_of["turn_out", PHASES, 0])

            def turn_tiles(src, i, bank):
                take(bank, "turned")
                for k in range(KC):
                    for t in range(2):
                        last = pe.transpose(by_tile(bank)[:, k, P * t:P * t + P], src[:, 2 * i + t, P * k:P * k + P],
                                            ident[:, :])
                last.then_inc(on["turned_full"], 1)

            def turn_attended(m, i, n, bank):
                pe.wait_ge(on["attended"], count.of("attended"))
                turn_tiles(attended, i, bank)

            def turn_normed(m, i, n, bank):
                pe.wait_ge(on["normed"], count.next("normed"))
                turn_tiles(normed_heads if n < m else normed_block, i, bank)

            def turn_leaves(m, i, n, bank):
                if i == 0 or alone(n):
                    count.add("level_done", LEVELS + 1)
                    pe.wait_ge(on["level_done"], count.of("level_done"))
                turn_tiles(leaf_probs[(LEVELS - 1) % 2], i, bank)

            def rows(turned, weight, i, bank, width, read):
                pe.wait_ge(on["turned"], count.of("turned"))
                take(bank, read)
                for t in range(2):
                    tile = slice(P * (2 * i + t), P * (2 * i + t + 1))
                    for k in range(KC):
                        last = pe.matmul(by_tile(bank)[:, t, 0:width], turned[:, k, tile], weight[:, k, 0:width],
                                         start=(k == 0), stop=(k == KC - 1))
                return last

            def project_out(m, i, n, bank):
                rows(turned_block, weights["b_o" if causal(m) else "a_o"], i, bank, D, "x_ready")\
                    .then_inc(on["added_full"], 1)

            def gates(m, i, n, bank):
                rows(turned_block, gate_w, i, bank, NODES, "gates").then_inc(on["gates_full"], 1)

            def mix(m, i, n, bank):
                rows(turned_block, leaf_w, i, bank, D, "x_ready")\
                    .then_inc(on["added_full"], 1)

            def values(m, i, n, bank):
                rows(turned_heads, weights["b_v" if causal(m) else "a_v"], i, bank, D, "values_ready")\
                    .then_inc(on["values_full"], 1)

            def heads(which):
                def step(m, i, n, bank):
                    weight = weights[("b_" if causal(m) else "a_") + which]
                    pe.wait_ge(on["turned"], count.of("turned"))
                    take(bank, "raw_ready")
                    for k in range(KC):
                        last = pe.matmul(bank[:, :], weight[:, k, P * i:P * i + P], turned_heads[:, k, :],
                                         start=(k == 0), stop=(k == KC - 1))
                    last.then_inc(on["heads_full"], 1)
                return step

            program(pe, count, core, dict(turn_attended=turn_attended, turn_normed=turn_normed,
                                          turn_leaves=turn_leaves, project_out=project_out, gates=gates, mix=mix,
                                          values=values, heads_k=heads("k"), heads_q=heads("q")),
                    opening, closing)


def by_pairs(weight):
    inner = weight.shape[1:]
    return np.moveaxis(weight.reshape((HEADS, PAIRS, 2) + inner), (0, 1, 2), (2, 1, 0)).reshape((D,) + inner)


def by_dims(weight):
    inner = weight.shape[1:]
    return np.moveaxis(weight.reshape((HEADS // 2, 2, DH) + inner), (0, 1, 2), (2, 0, 1)).reshape((D,) + inner)


def rope_tables():
    rates = np.float32(THETA) ** (-(np.float32(2.0) * np.arange(PAIRS, dtype=np.float32)) / np.float32(DH))
    angles = np.repeat(rates.astype(np.float32), HEADS)[:, None] * np.arange(T, dtype=np.float32)[None, :]
    return np.cos(angles).astype(np.float32), np.sin(angles).astype(np.float32)


def kernel(**inputs):
    import concourse.bacc as bacc
    from concourse.bass_utils import run_bass_kernel_spmd

    a = {name[3:]: np.asarray(value) for name, value in inputs.items()}
    qkv, qkv_b = a["attn_a_qkv_w"], a["attn_a_qkv_b"]
    cos, sin = rope_tables()
    arrays = dict(
        x=a["attn_a_x"],
        a_q=by_dims(qkv[:D]).T, a_k=by_dims(qkv[D:2 * D]).T, a_v=qkv[2 * D:].T, a_o=a["attn_a_out_w"].T,
        a_q_bias=by_dims(qkv_b[:D]).reshape(2, P).T, a_k_bias=by_dims(qkv_b[D:2 * D]).reshape(2, P).T,
        a_v_bias=qkv_b[2 * D:], a_o_bias=a["attn_a_out_b"],
        b_q=by_pairs(a["attn_b_Wq"]).T, b_k=by_pairs(a["attn_b_Wk"]).T, b_v=a["attn_b_Wv"].T, b_o=a["attn_b_Wo"].T,
        ffn_q=a["ffn_Wq"], routers=a["ffn_routers"].T, leaf_values=a["ffn_leaf_values"].T, ffn_o=a["ffn_Wout_w"].T,
        ffn_bias=a["ffn_Wout_b"], cosine=cos, sine=sin,
    )
    arrays = {f"in_{name}": np.ascontiguousarray(value) for name, value in arrays.items()}
    nc = bacc.Bacc("TRN2", target_bir_lowering=False, num_devices=1)
    w = {n[3:]: nc.dram_tensor(n, v.shape, F32, kind="ExternalInput").ap() for n, v in arrays.items()}
    out = nc.dram_tensor("out", (BATCH, T, D), F32, kind="ExternalOutput").ap()
    build(nc, w.pop("x"), w, out)
    return run_bass_kernel_spmd(nc, [arrays], core_ids=[0]).results[0]["out"]
```
